# Optimizing a Trainium2 kernel written in Bass

```python
import numpy as np
import jax
import jax.numpy as jnp

def _softmax(x, axis=-1):
    return jax.nn.softmax(x, axis=axis)

def _gelu(x):
    return jax.nn.gelu(x, approximate=True)

def _silu(x):
    return jax.nn.silu(x)

def _sigmoid(x):
    return jax.nn.sigmoid(x)

def _layernorm(x, axis=-1, eps=1e-05):
    m = jnp.mean(x, axis=axis, keepdims=True)
    v = jnp.var(x, axis=axis, keepdims=True)
    return (x - m) / jnp.sqrt(v + eps)

def _scatter_add(tgt, idx, src, axis=0):
    return tgt.at[idx].add(src)

def _segment_sum(src, seg, n):
    return jax.ops.segment_sum(src, seg, n)
kernel_name = 'mk_gnn_ffn_d1_gnn_r8_28f693'

def setup_inputs(seed: int=0):
    np.random.seed(seed)
    _w = jnp.asarray

    def _rec_inputs():
        import jax
        import jax.numpy as jnp
        _gk = jax.random.key(seed)
        x = -0.0002117 + 1 * jax.random.normal(jax.random.fold_in(_gk, 1), (6250, 256), jnp.float32)
        src = jax.random.randint(jax.random.fold_in(_gk, 2), (100000,), 0, 6250, jnp.int32)
        dst = jax.random.randint(jax.random.fold_in(_gk, 3), (100000,), 0, 6250, jnp.int32)
        _o = jnp.argsort(dst, stable=True)
        src = src[_o]
        dst = dst[_o]
        edge_type_500 = jax.random.randint(jax.random.fold_in(_gk, 12), (100000,), 0, 500, jnp.int32)
        return (x, src, dst, edge_type_500)
    x, src, dst, edge_type_500 = _rec_inputs()

    def _L0_gnn_setup():
        import jax, jax.numpy as jnp
        import numpy as np
        G = (1.0, 1.0)

        def to_hypercomplex(x, n_blades):
            return x.reshape(*x.shape[:-1], n_blades, -1).swapaxes(-2, -1)

        def clifford_kernel_2d(w, g):
            g0, g1 = g
            k0 = jnp.concatenate([w[0], g0 * w[1], g1 * w[2], -g0 * g1 * w[3]], axis=1)
            k1 = jnp.concatenate([w[1], w[0], -g1 * w[3], g1 * w[2]], axis=1)
            k2 = jnp.concatenate([w[2], g0 * w[3], w[0], -g0 * w[1]], axis=1)
            k3 = jnp.concatenate([w[3], w[2], w[1], w[0]], axis=1)
            return jnp.concatenate([k0, k1, k2, k3], axis=0)

        def clifford_linear(x, w, b, g=G):
            N = x.shape[0]
            k = clifford_kernel_2d(w, g)
            xf = x.swapaxes(-2, -1).reshape(N, -1)
            out = xf @ k.T + b.reshape(-1)
            C_out = w.shape[1]
            return out.reshape(N, 4, C_out).swapaxes(-2, -1)
        key = jax.random.key(seed)
        ks = jax.random.split(key, 10)
        N, E, R, emb_dim = (12500, 75000, 500, 256)
        C = emb_dim // 4
        s = 0.05
        return {'h': jax.random.normal(ks[0], (N, emb_dim), jnp.float32), 'edge_index': jax.random.randint(ks[1], (2, E), 0, N, jnp.int64), 'edge_type': jax.random.randint(ks[2], (E,), 0, R, jnp.int64), 'relation_emb': jax.random.normal(ks[3], (R, emb_dim), jnp.float32), 'msg_w': jax.random.normal(ks[4], (4, C, C), jnp.float32) * s, 'msg_b': jax.random.normal(ks[5], (4, C), jnp.float32) * s, 'upd_w': jax.random.normal(ks[6], (4, C, C), jnp.float32) * s, 'upd_b': jax.random.normal(ks[7], (4, C), jnp.float32) * s, 'gate_w': jax.random.normal(ks[8], (1, emb_dim), jnp.float32) * s, 'gate_b': jax.random.normal(ks[9], (1,), jnp.float32) * s}
    _L0_gnn_all = _L0_gnn_setup()
    _L0_gnn_in = {k: v for k, v in _L0_gnn_all.items() if k in ('relation_emb', 'msg_w', 'msg_b', 'upd_w', 'upd_b', 'gate_w', 'gate_b')}
    del _L0_gnn_all

    def _L0_ffn_setup():
        import jax, jax.numpy as jnp
        import numpy as np
        BN_EPS = 0.001

        def _bn(h, g, b, m, v):
            return g * (h - m) * jax.lax.rsqrt(v + BN_EPS) + b
        key = jax.random.key(seed)
        ks = jax.random.split(key, 8)
        B, F, Df = (256, 64, 256)
        E, H, D = (8, 256, 256)
        s1 = 1.0 / np.sqrt(Df)
        s2 = 1.0 / np.sqrt(H)
        return {'x': jax.random.normal(ks[0], (B, F, Df), jnp.float32), 'Wr': jax.random.normal(ks[1], (Df, E), jnp.float32) * s1, 'br': jnp.zeros((E,), jnp.float32), 'W1': jax.random.normal(ks[2], (E, Df, H), jnp.float32) * s1, 'b1': jnp.zeros((E, H), jnp.float32), 'g1': jnp.ones((E, H), jnp.float32), 'be1': jnp.zeros((E, H), jnp.float32), 'm1': jnp.zeros((E, H), jnp.float32), 'v1': jnp.ones((E, H), jnp.float32), 'W2': jax.random.normal(ks[3], (E, H, H), jnp.float32) * s2, 'b2': jnp.zeros((E, H), jnp.float32), 'g2': jnp.ones((E, H), jnp.float32), 'be2': jnp.zeros((E, H), jnp.float32), 'm2': jnp.zeros((E, H), jnp.float32), 'v2': jnp.ones((E, H), jnp.float32), 'Wo': jax.random.normal(ks[4], (E, H, D), jnp.float32) * s2, 'bo': jnp.zeros((E, D), jnp.float32)}
    _L0_ffn_all = _L0_ffn_setup()
    _L0_ffn_in = {k: v for k, v in _L0_ffn_all.items() if k in ('Wr', 'br', 'W1', 'b1', 'g1', 'be1', 'm1', 'v1', 'W2', 'b2', 'g2', 'be2', 'm2', 'v2', 'Wo', 'bo')}
    del _L0_ffn_all
    return {'x': x, 'src': src, 'dst': dst, 'edge_type_500': edge_type_500, 'L0_gnn_relation_emb': _L0_gnn_in['relation_emb'], 'L0_gnn_msg_w': _L0_gnn_in['msg_w'], 'L0_gnn_msg_b': _L0_gnn_in['msg_b'], 'L0_gnn_upd_w': _L0_gnn_in['upd_w'], 'L0_gnn_upd_b': _L0_gnn_in['upd_b'], 'L0_gnn_gate_w': _L0_gnn_in['gate_w'], 'L0_gnn_gate_b': _L0_gnn_in['gate_b'], 'L0_ffn_Wr': _L0_ffn_in['Wr'], 'L0_ffn_br': _L0_ffn_in['br'], 'L0_ffn_W1': _L0_ffn_in['W1'], 'L0_ffn_b1': _L0_ffn_in['b1'], 'L0_ffn_g1': _L0_ffn_in['g1'], 'L0_ffn_be1': _L0_ffn_in['be1'], 'L0_ffn_m1': _L0_ffn_in['m1'], 'L0_ffn_v1': _L0_ffn_in['v1'], 'L0_ffn_W2': _L0_ffn_in['W2'], 'L0_ffn_b2': _L0_ffn_in['b2'], 'L0_ffn_g2': _L0_ffn_in['g2'], 'L0_ffn_be2': _L0_ffn_in['be2'], 'L0_ffn_m2': _L0_ffn_in['m2'], 'L0_ffn_v2': _L0_ffn_in['v2'], 'L0_ffn_Wo': _L0_ffn_in['Wo'], 'L0_ffn_bo': _L0_ffn_in['bo']}

def reference(x, src, dst, edge_type_500, L0_gnn_relation_emb, L0_gnn_msg_w, L0_gnn_msg_b, L0_gnn_upd_w, L0_gnn_upd_b, L0_gnn_gate_w, L0_gnn_gate_b, L0_ffn_Wr, L0_ffn_br, L0_ffn_W1, L0_ffn_b1, L0_ffn_g1, L0_ffn_be1, L0_ffn_m1, L0_ffn_v1, L0_ffn_W2, L0_ffn_b2, L0_ffn_g2, L0_ffn_be2, L0_ffn_m2, L0_ffn_v2, L0_ffn_Wo, L0_ffn_bo):
    import jax
    import jax.numpy as jnp

    def _L0_gnn_ref(h, edge_index, edge_type, relation_emb, msg_w, msg_b, upd_w, upd_b, gate_w, gate_b):
        import jax, jax.numpy as jnp
        import numpy as np
        G = (1.0, 1.0)

        def to_hypercomplex(x, n_blades):
            return x.reshape(*x.shape[:-1], n_blades, -1).swapaxes(-2, -1)

        def clifford_kernel_2d(w, g):
            g0, g1 = g
            k0 = jnp.concatenate([w[0], g0 * w[1], g1 * w[2], -g0 * g1 * w[3]], axis=1)
            k1 = jnp.concatenate([w[1], w[0], -g1 * w[3], g1 * w[2]], axis=1)
            k2 = jnp.concatenate([w[2], g0 * w[3], w[0], -g0 * w[1]], axis=1)
            k3 = jnp.concatenate([w[3], w[2], w[1], w[0]], axis=1)
            return jnp.concatenate([k0, k1, k2, k3], axis=0)

        def clifford_linear(x, w, b, g=G):
            N = x.shape[0]
            k = clifford_kernel_2d(w, g)
            xf = x.swapaxes(-2, -1).reshape(N, -1)
            out = xf @ k.T + b.reshape(-1)
            C_out = w.shape[1]
            return out.reshape(N, 4, C_out).swapaxes(-2, -1)
        n_blades = 4
        num_nodes = h.shape[0]
        h_hc = to_hypercomplex(h, n_blades)
        r_hc = to_hypercomplex(relation_emb, n_blades)
        src, dst = (edge_index[0], edge_index[1])
        h_src = h_hc[src]
        r_uv = r_hc[edge_type]
        m = clifford_linear(h_src * r_uv, msg_w, msg_b)
        gate = jax.nn.sigmoid(r_uv.reshape(r_uv.shape[0], -1) @ gate_w.T + gate_b)
        m = m * gate[:, :, None]
        ones = jnp.ones_like(src, dtype=jnp.float32)
        deg_src = jax.ops.segment_sum(ones, src, num_segments=num_nodes)
        deg_dst = jax.ops.segment_sum(ones, dst, num_segments=num_nodes)
        norm = jnp.maximum(deg_src[src] * deg_dst[dst], 1.0) ** (-0.5)
        m = m * norm[:, None, None]
        h_agg = jax.ops.segment_sum(m, dst, num_segments=num_nodes)
        h_out = clifford_linear(h_hc + h_agg, upd_w, upd_b)
        return h_out.reshape(num_nodes, -1)

    def _L0_ffn_ref(x, Wr, br, W1, b1, g1, be1, m1, v1, W2, b2, g2, be2, m2, v2, Wo, bo):
        import jax, jax.numpy as jnp
        import numpy as np
        BN_EPS = 0.001

        def _bn(h, g, b, m, v):
            return g * (h - m) * jax.lax.rsqrt(v + BN_EPS) + b
        feat = jnp.mean(x, axis=0)
        w = jax.nn.softmax(feat @ Wr + br, axis=-1)
        h = jnp.einsum('bfd,edh->bfeh', x, W1) + b1
        h = jax.nn.relu(_bn(h, g1, be1, m1, v1))
        h = jnp.einsum('bfeh,ehk->bfek', h, W2) + b2
        h = jax.nn.relu(_bn(h, g2, be2, m2, v2))
        y = jnp.einsum('bfeh,ehd->bfed', h, Wo) + bo
        return jnp.einsum('bfed,fe->bfd', y, w)
    edge_index = jnp.stack([src, dst])
    x = x + _L0_gnn_ref(_layernorm(x, axis=-1), edge_index, edge_type_500, L0_gnn_relation_emb, L0_gnn_msg_w, L0_gnn_msg_b, L0_gnn_upd_w, L0_gnn_upd_b, L0_gnn_gate_w, L0_gnn_gate_b)
    x = x + _L0_ffn_ref(_layernorm(x, axis=-1)[None], L0_ffn_Wr, L0_ffn_br, L0_ffn_W1, L0_ffn_b1, L0_ffn_g1, L0_ffn_be1, L0_ffn_m1, L0_ffn_v1, L0_ffn_W2, L0_ffn_b2, L0_ffn_g2, L0_ffn_be2, L0_ffn_m2, L0_ffn_v2, L0_ffn_Wo, L0_ffn_bo)[0]
    return x

_drawn_inputs = setup_inputs


def setup_inputs(seed=0):
    import zlib

    import numpy as np

    out = dict(_drawn_inputs(seed))
    spreads = {'L0_ffn_br': (0.0, 0.301),
     'L0_ffn_b1': (0.0, 0.401),
     'L0_ffn_g1': (1.0, 0.2),
     'L0_ffn_be1': (0.0, 0.411),
     'L0_ffn_m1': (0.0, 0.402),
     'L0_ffn_v1': (1.0, 0.6),
     'L0_ffn_b2': (0.0, 0.286),
     'L0_ffn_g2': (1.0, 0.2),
     'L0_ffn_be2': (0.0, 0.299),
     'L0_ffn_m2': (0.0, 0.297),
     'L0_ffn_v2': (1.0, 0.6),
     'L0_ffn_bo': (0.0, 0.1)}
    factors = {'L0_gnn_msg_b': 3.443}
    for name, (base, spread) in spreads.items():
        noise = np.random.default_rng([zlib.crc32(name.encode()), seed]).standard_normal(out[name].shape)
        drawn = base * np.exp(spread * noise) if base else spread * noise
        out[name] = jnp.asarray(drawn.astype(out[name].dtype))
    for name, factor in factors.items():
        out[name] = (out[name] * factor).astype(out[name].dtype)
    return out
```

```python
from contextlib import ExitStack

import numpy as np
import concourse.bass as bass
from concourse import mybir

P = 128
D = 256
DX = 260
NE = 8
W = 64
SB = 4
GT = 4
GS = 16
LEAD = 4
LN_EPS = 1e-5
BN_EPS = 1e-3
NEG = ((0, 3), (1, 2), (2, 3))


def sizes(n, e):
    nt = -(-n // P)
    ng = -(-nt // GT)
    nsb = GS * (ng - 2) + GS + LEAD
    assert nt == GT * (ng - 1) + 1 and 0 <= nsb * SB * P - e, (nt, ng, nsb, e)
    return nt, ng, nsb


def build(nc, a, out, n, e, nrel):
    fp32, i32, bf16 = mybir.dt.float32, mybir.dt.int32, mybir.dt.bfloat16
    ALU, ACT, AX = mybir.AluOpType, mybir.ActivationFunctionType, mybir.AxisListType
    NT, NG, NSB = sizes(n, e)
    NB = NSB * SB
    NBI = NB + GS * SB
    NP = NT * P
    AW = NP + W
    NW = NP // W
    RT = nrel // 4
    T = GT * P
    HB = max(h for h in range(1, 17) if NB % (2 * h) == 0)
    ds = bass.ds

    htab = nc.dram_tensor("h_table", [NP, DX], fp32, kind="Internal").ap()
    rtab = nc.dram_tensor("r_table", [nrel + 1, DX], fp32, kind="Internal").ap()

    ctx = ExitStack()
    with ctx:
        def sb(name, shape, dt=fp32):
            return ctx.enter_context(nc.sbuf_tensor(name, shape, dt))

        def sem(name):
            return ctx.enter_context(nc.semaphore(name))

        big = sb("big", [P, 3 * AW])
        aggT = big[:, 0:2 * AW].rearrange("p (k c) -> p k c", k=2)
        aggC = big[0:2, 2 * AW:3 * AW]
        xall = big[:, 0:NT * DX].rearrange("p (t c) -> p t c", t=NT)
        w1, w2, wo = (sb(x, [P, NE, 2, D]) for x in ("w1", "w2", "wo"))
        H = sb("H", [P, 4, SB * DX])
        R = sb("R", [P, 2, SB * DX])
        src = sb("src", [P, NBI], i32)
        typ = sb("typ", [P, NBI], i32)
        idx = sb("idx", [P, 2, 2, GS * SB // 2], i32)
        dloc = sb("dloc", [P, NB])
        dwin = sb("dwin", [P, SB])
        S = sb("S", [P, 2, SB, W])
        Psb = sb("Psb", [W, 2, DX])
        xg = sb("xg", [P, GT, D])
        acc = sb("acc", [P, GT, D])
        hg = sb("hg", [P, GT, D])
        hT = sb("hT", [P, 2, T])
        aT = sb("aT", [P, 2, T])
        aC = sb("aC", [2, T])
        h1 = sb("h1", [P, 2, 2, T])
        h2 = sb("h2", [P, 2, 2, T])
        UT = sb("UT", [P, 2, D])
        W2T = sb("W2T", [P, 2, D])
        umb = sb("umb", [2, D])
        wr = sb("wr", [P, 2, NE])
        at0 = 2 * AW + NT * DX % P + P
        bo = big[32:32 + NE, at0:at0 + D]
        wT = big[32:32 + NE, at0 + D:at0 + D + T]
        rows = sb("rows", [1, D + NE + P])
        ub, br, ones = rows[:, 0:D], rows[:, D:D + NE], rows[:, D + NE:]
        base_i = big[96:97, at0:at0 + NSB].bitcast(i32)
        bns = sb("bns", [P, 2, 2, NE * 2])
        ident = sb("ident", [P, P])
        iota_w = sb("iota_w", [P, W])
        sel = sb("sel", [2, 1])
        mean = sb("mean", [P, NT + GT])
        rstd = sb("rstd", [P, NT + GT])
        flag = sb("flag", [P, 4])
        flag_i = sb("flag_i", [1, 1], i32)
        gm = sb("gm", [P, 2, GT])
        dd = sb("dd", [P, GT])
        st = sb("st", [P, GT, 6])
        mv = sb("mv", [P, GT, 2])
        rs = sb("rs", [P, GT])
        mx = sb("mx", [P, GT])
        wg = sb("wg", [P, GT, NE])
        oh_lo = [h1[:, i, :, :].rearrange("p a b -> p (a b)").bitcast(bf16)[:, 0:HB * P]
                 .rearrange("p (b c) -> p b c", b=HB) for i in range(2)]
        oh_hi = [h2[:, 0, i, :].bitcast(bf16)[:, 0:HB * NT]
                 .rearrange("p (b c) -> p b c", b=HB) for i in range(2)]
        hflat = H[:, :, :].rearrange("p a b -> p (a b)")
        lo_f = hflat[:, 0:NB]
        hi_f = hflat[:, NB:2 * NB]
        lo_i = hflat[:, 2 * NB:3 * NB].bitcast(i32)
        hi_i = hflat[:, 3 * NB:4 * NB].bitcast(i32)
        rflat = R[:, :, :].rearrange("p a b -> p (a b)")
        rext = rflat[:, 0:4 * DX].rearrange("p (k c) -> p k c", k=4)
        dst_i = rflat[:, 4 * DX:4 * DX + NB].bitcast(i32)
        rel = xg
        bn = h2[:, 1, 0, 0:10 * NE * 2].rearrange("p (l q c) -> p l q c", l=2, q=5)
        ones0 = h2[0:1, 1, 1, 0:P]
        gwb = hg[:, 0, :]
        rprod = hg[:, 1, :]
        zrow = acc[0:1, 2:4, :].rearrange("p a b -> p (a b)")[:, 0:DX]
        km = aT
        mb = acc[:, 0, 0:2]
        gbc = acc[:, 0, 2:3]
        gate = acc[:, 0, 4:8]
        egate = acc[:, 0, 8:12]
        iota_b = hT[:, 0, :].bitcast(bf16)[:, 0:P]
        iota_f = hT[:, 1, 0:P]
        sq = hg[:, 3, :]
        ssum = hT[:, 1, P:P + NT]
        ssq = hT[:, 1, 2 * P:2 * P + NT]
        dsr = acc[:, 1, 0:NT]
        hsc = acc[:, 1, 64:64 + NT]
        hbi = acc[:, 1, 128:128 + NT]

        def bank(name):
            return ctx.enter_context(nc.psum_tensor(name, [P, 512], fp32))

        Z = [bank("z0"), bank("z1")]
        Y = [bank("y0"), bank("y1")]
        PA = [bank("pa0"), bank("pa1")]
        PT = [bank("pt0"), bank("pt1")]

        ld_idx, ld_dst, ld_rel, ld_cl, ld_bn, ld_ffn = (sem(x) for x in
            ("ld_idx", "ld_dst", "ld_rel", "ld_clifford", "ld_bn", "ld_experts"))
        ld_x = sem("ld_x")
        ld_typ = sem("ld_typ")
        consts, iotas = sem("consts"), sem("iotas")
        bins, oh_lo_done, oh_hi_done, oh_used, deg_done = (sem(x) for x in
            ("bins", "oh_lo_done", "oh_hi_done", "oh_used", "deg_done"))
        stats, ln_var, ln_sd, hscaled, tab_h, tab_r, r_ready, z_ready = (sem(x) for x in
            ("stats", "ln_var", "ln_sd", "hscaled", "tab_h", "tab_r", "r_ready", "z_ready"))
        gsum, gexp, cl_ready, w2_mm, base_mm, base_row, bn_in, bn_sd, ds_in, ds_sd = (sem(x) for x in
            ("gate_sum", "gate_exp", "clifford_ready", "w2_mm", "base_mm", "base_row",
             "bn_in", "bn_sd", "ds_in", "ds_sd"))
        z_dve, flag_in, flag_all, flag_done, tabs = (sem(x) for x in
            ("startup_dve", "flag_in", "flag_all", "flag_done", "tables"))
        act_own, pool_own, z_row = sem("startup_act"), sem("startup_pool"), sem("zero_row")
        HIT = NB // (2 * HB)
        assert HIT * 2 * HB == NB
        XC = 7
        NC = NT // XC if NT % XC == 0 else 1
        XN = NT // NC

        with nc.Block() as block:
            @block.sync
            def _(sp):
                sp.dma_start(src[:, :], a["src"]).then_inc(ld_idx, 16)
                sp.dma_start(dst_i, a["dst"]).then_inc(ld_dst, 16)
                sp.dma_start(rel[0:RT, :, :], a["rel"].rearrange("(k p) d -> p k d", k=4)).then_inc(ld_rel, 16)
                sp.dma_start(gwb[0:RT, :], a["gw"].partition_broadcast(RT)).then_inc(ld_rel, 16)
                sp.dma_start(gbc[0:RT, :], a["gb"].partition_broadcast(RT)).then_inc(ld_rel, 16)
                xv = a["x"].rearrange("(t p) d -> p t d", p=P)
                for c in range(NC):
                    sp.dma_start(xall[:, c * XN:(c + 1) * XN, 0:D], xv[:, c * XN:(c + 1) * XN, :]).then_inc(ld_x, 16)
                sp.dma_start(typ[:, :], a["typ"]).then_inc(ld_typ, 16)
                sp.dma_start(km[:, :, 0:D], a["km"].rearrange("(k p) d -> p k d", p=P)).then_inc(ld_cl, 16)
                sp.dma_start(UT[:, :, :], a["ut"].rearrange("(k p) d -> p k d", p=P)).then_inc(ld_cl, 16)
                sp.dma_start(mb, a["mb"]).then_inc(ld_cl, 16)
                sp.dma_start(ub, a["ub"]).then_inc(ld_cl, 16)
                sp.dma_start(bn[:, :, :, :], a["bn"]).then_inc(ld_bn, 16)
                sp.dma_start(wr[:, :, :], a["wr"].rearrange("(k p) d -> p k d", p=P)).then_inc(ld_ffn, 16)
                sp.dma_start(br, a["br"]).then_inc(ld_ffn, 16)
                sp.dma_start(bo, a["bo"]).then_inc(ld_ffn, 16)
                for t, name in ((w1, "w1"), (w2, "w2"), (wo, "wo")):
                    for i in range(NE):
                        sp.dma_start(t[:, i, :, :], a[name][i, :, :].rearrange("(k p) d -> p k d", p=P)).then_inc(ld_ffn, 16)
                sp.wait_ge(r_ready, 1)
                sp.dma_start(rtab[0:nrel, :].rearrange("(k p) c -> p k c", k=4), rext[0:RT, :, :]).then_inc(tab_r, 16)
                sp.wait_ge(z_row, 1)
                sp.dma_start(rtab[nrel:nrel + 1, :], zrow).then_inc(tab_r, 16)
                hv = htab.rearrange("(t p) c -> p t c", p=P)
                for c in range(NC):
                    sp.wait_ge(hscaled, c + 1)
                    sp.dma_start(hv[:, c * XN:(c + 1) * XN, :], xall[:, c * XN:(c + 1) * XN, :]).then_inc(tab_h, 16)
                sp.wait_ge(tab_r, 32)
                sp.wait_ge(tab_h, 16 * NC)
                sp.wait_ge(ld_ffn, 16 * (3 + 3 * NE))
                sp.wait_ge(ld_idx, 16)
                sp.wait_ge(ld_typ, 16)

            @block.gpsimd
            def _(pool):
                pool.iota(iota_f, pattern=[[1, P]], base=0, channel_multiplier=0,
                          allow_small_or_imprecise_dtypes=True).then_inc(iotas, 1)
                pool.memset(ident[:, :], 0.0).then_inc(pool_own, 1)
                pool.wait_ge(pool_own, 1)
                pool.affine_select(out=ident[:, :], in_=ident[:, :], compare_op=ALU.not_equal, fill=1.0,
                                   base=0, pattern=[[-1, P]], channel_multiplier=1).then_inc(consts, 1)
                pool.memset(xall[:, :, D:DX], 0.0).then_inc(pool_own, 1)
                pool.wait_ge(pool_own, 2)
                pool.memset(xall[:, :, D + 1:D + 2], 1.0).then_inc(consts, 1)
                pool.wait_ge(flag_in, 1)
                pool.partition_all_reduce(flag[:, 1:2], flag[:, 0:1], P, bass.bass_isa.ReduceOp.max).then_inc(flag_all, 1)

            @block.scalar
            def _(act):
                own = [0]

                def link(ins):
                    own[0] += 1
                    ins.then_inc(act_own, 1)
                    act.wait_ge(act_own, own[0])

                for c in range(NC):
                    act.wait_ge(ld_x, 16 * NC)
                    for t in range(c * XN, (c + 1) * XN):
                        last = nc.scalar.activation(sq, xall[:, t, 0:D], ACT.Copy, accum_out=ssum[:, t:t + 1])
                        link(last)
                act.mul(mean[:, 0:NT], ssum, -1.0 / D).then_inc(stats, 1)
                act.wait_ge(stats, 1)
                for t in range(NT):
                    link(nc.scalar.activation(sq, xall[:, t, 0:D], ACT.Square, bias=mean[:, t:t + 1],
                                              accum_out=ssq[:, t:t + 1]))
                act.sem_inc(stats, 1)
                act.wait_ge(ln_var, 1)
                nc.scalar.activation(rstd[:, 0:NT], rstd[:, 0:NT], ACT.Sqrt).then_inc(ln_sd, 1)
                act.wait_ge(ds_in, 1)
                nc.scalar.activation(dsr, dsr, ACT.Sqrt).then_inc(ds_sd, 1)
                act.wait_ge(bn_in, 1)
                nc.scalar.activation(bns[:, :, 0, :], bns[:, :, 0, :], ACT.Sqrt).then_inc(bn_sd, 1)
                act.wait_ge(gsum, 1)
                nc.scalar.activation(egate[0:RT, :], gate[0:RT, :], ACT.Exp, scale=-1.0).then_inc(gexp, 1)

            @block.tensor
            def _(pe):
                pe.wait_ge(oh_lo_done, 1)
                with pe.Fori(0, HIT) as i:
                    for h in range(2):
                        pe.wait_ge(oh_lo_done, i * 2 + h + 2)
                        for b in range(HB):
                            last = pe.matmul(Y[0][:, 0:NT], oh_lo[h][:, b, :], oh_hi[h][:, b, :],
                                             start=False, stop=True, skip_group_check=True)
                        last.then_inc(oh_used, 1)
                pe.wait_ge(base_row, 1)
                pe.matmul(Z[0][:, 0:NSB], ones0, dloc[0:1, 0:NB:SB],
                          start=True, stop=True).then_inc(base_mm, 1)
                pe.wait_ge(cl_ready, 1)
                for m in range(2):
                    for k in range(2):
                        pe.matmul(Z[1][:, m * D:(m + 1) * D], km[:, k, m * P:(m + 1) * P], UT[:, k, :],
                                  start=k == 0, stop=k == 1)
                for k in range(2):
                    last = pe.matmul(Y[1][0:1, 0:D], mb[:, k:k + 1], UT[:, k, :], start=k == 0, stop=k == 1)
                last.then_inc(w2_mm, 1)

            @block.vector
            def _(dve):
                own = [0]

                def link(ins):
                    own[0] += 1
                    ins.then_inc(z_dve, 1)
                    dve.wait_ge(z_dve, own[0])

                v = nc.vector
                dve.wait_ge(ld_idx, 16)
                dve.wait_ge(iotas, 1)
                v.memset(ones, 1.0)
                v.memset(ones0, 1.0)
                v.tensor_copy(iota_b, iota_f)
                v.tensor_copy(iota_w[:, :], iota_f[:, 0:W])
                v.memset(zrow, 0.0).then_inc(z_row, 1)
                v.tensor_scalar(lo_i, src[:, 0:NB], P - 1, None, ALU.bitwise_and)
                link(v.tensor_scalar(hi_i, src[:, 0:NB], 7, None, ALU.logical_shift_right))
                v.tensor_copy(lo_f, lo_i)
                v.tensor_copy(hi_f, hi_i).then_inc(bins, 1)
                v.memset(Y[0][:, 0:NT], 0.0).then_inc(oh_lo_done, 1)
                dve.sem_inc(oh_used, 2)
                dve.wait_ge(bins, 1)
                with dve.Fori(0, HIT) as i:
                    for h in range(2):
                        dve.wait_ge(oh_used, i * 2 + h + 1)
                        v.tensor_tensor(
                            oh_hi[h], hi_f[:, ds(i * (2 * HB) + h * HB, HB)].unsqueeze(2).to_broadcast([P, HB, NT]),
                            iota_f[:, 0:NT].unsqueeze(1).to_broadcast([P, HB, NT]), ALU.is_equal)
                        for b in range(HB):
                            last = v.tensor_scalar(oh_lo[h][:, b, :], iota_b,
                                                   lo_f[:, ds(i * (2 * HB) + (h * HB + b), 1)], None, ALU.is_equal)
                        last.then_inc(oh_lo_done, 1)
                dve.wait_ge(stats, 2)
                link(v.tensor_scalar(rstd[:, 0:NT], ssq, 1.0 / D, LN_EPS, ALU.mult, ALU.add))
                v.tensor_copy(rstd[:, 0:NT], rstd[:, 0:NT]).then_inc(ln_var, 1)
                dve.wait_ge(oh_used, 2 + 2 * HIT)
                v.tensor_scalar(dsr, Y[0][:, 0:NT], 1.0, None, ALU.max).then_inc(ds_in, 1)
                dve.wait_ge(ld_bn, 16)
                v.tensor_scalar(bns[:, :, 0, :], bn[:, :, 4, :], BN_EPS, None, ALU.add).then_inc(bn_in, 1)
                dve.wait_ge(ds_sd, 1)
                link(v.reciprocal(dsr, dsr))
                dve.wait_ge(ln_sd, 1)
                link(v.reciprocal(rstd[:, 0:NT], rstd[:, 0:NT]))
                link(v.tensor_tensor(hsc, rstd[:, 0:NT], dsr, ALU.mult))
                v.tensor_tensor(hbi, mean[:, 0:NT], hsc, ALU.mult)
                dve.wait_ge(consts, 2)
                link(v.tensor_copy(xall[:, :, D:D + 1].rearrange("p t o -> p (t o)"), dsr))
                for t in range(NT):
                    last = v.tensor_scalar(xall[:, t, 0:D], xall[:, t, 0:D], hsc[:, t:t + 1], hbi[:, t:t + 1],
                                           ALU.mult, ALU.add)
                    if t % XN == XN - 1:
                        last.then_inc(hscaled, 1)
                dve.wait_ge(bn_sd, 1)
                link(v.reciprocal(bns[:, :, 0, :], bns[:, :, 0, :]))
                link(v.tensor_tensor(bns[:, :, 0, :], bns[:, :, 0, :], bn[:, :, 1, :], ALU.mult))
                link(v.tensor_tensor(bns[:, :, 1, :], bn[:, :, 0, :], bn[:, :, 3, :], ALU.subtract))
                link(v.tensor_tensor(bns[:, :, 1, :], bns[:, :, 1, :], bns[:, :, 0, :], ALU.mult))
                link(v.tensor_tensor(bns[:, :, 1, :], bns[:, :, 1, :], bn[:, :, 2, :], ALU.add))
                dve.wait_ge(ld_rel, 48)
                for k in range(4):
                    link(v.tensor_tensor(rprod[0:RT, :], rel[0:RT, k, :], gwb[0:RT, :], ALU.mult))
                    link(v.reduce_sum(gate[0:RT, k:k + 1], rprod[0:RT, :], AX.X))
                v.tensor_scalar(gate[0:RT, :], gate[0:RT, :], gbc[0:RT, :], None, ALU.add).then_inc(gsum, 1)
                dve.wait_ge(gexp, 1)
                link(v.tensor_scalar(egate[0:RT, :], egate[0:RT, :], 1.0, None, ALU.add))
                link(v.reciprocal(gate[0:RT, :], egate[0:RT, :]))
                link(v.memset(rext[0:RT, :, D:DX], 0.0))
                v.memset(rext[0:RT, :, D + 1:D + 2], 1.0)
                v.tensor_copy(rext[0:RT, :, D:D + 1].rearrange("p k o -> p (k o)"), gate[0:RT, :])
                for k in range(4):
                    last = v.tensor_scalar(rext[0:RT, k, 0:D], rel[0:RT, k, :], gate[0:RT, k:k + 1], None, ALU.mult)
                last.then_inc(r_ready, 1)
                dve.wait_ge(ld_cl, 64)
                for b, q in NEG:
                    kb = km[(b % 2) * 64:(b % 2) * 64 + 64, b // 2, q * 64:q * 64 + 64]
                    v.tensor_scalar(kb, kb, -1.0, None, ALU.mult)
                    us = UT[(q % 2) * 64:(q % 2) * 64 + 64, q // 2, b:D:4]
                    last = v.tensor_scalar(us, us, -1.0, None, ALU.mult)
                last.then_inc(cl_ready, 1)
                dve.wait_ge(ld_dst, 16)
                v.tensor_copy(dloc[:, :], dst_i).then_inc(base_row, 1)
                v.tensor_copy(base_i, dst_i[0:1, 0:NB:SB])
                dve.wait_ge(base_row, 1)
                tmp = hflat[:, 0:NB]
                viol = hflat[:, NB:2 * NB]
                link(v.memset(tmp, 0.0))
                for g in range(NG - 2):
                    lo = (GS * (g + 1) + LEAD - 2) * SB
                    hi = (GS * (g + 2) + LEAD - 2) * SB if g < NG - 3 else NB
                    link(v.memset(tmp[:, lo:hi], float(T * (g + 1))))
                link(v.tensor_tensor(viol, tmp, dloc[:, :], ALU.subtract))
                dve.wait_ge(base_mm, 1)
                link(v.tensor_tensor(dloc[:, :].rearrange("p (s b) -> p s b", b=SB),
                                     dloc[:, :].rearrange("p (s b) -> p s b", b=SB),
                                     Z[0][:, 0:NSB].unsqueeze(2).to_broadcast([P, NSB, SB]), ALU.subtract))
                link(v.tensor_scalar(tmp, dloc[:, :], -1.0, None, ALU.mult))
                link(v.tensor_tensor(viol, viol, tmp, ALU.max))
                link(v.tensor_scalar(tmp, dloc[:, :], float(1 - W), None, ALU.add))
                link(v.tensor_tensor(viol, viol, tmp, ALU.max))
                v.reduce_max(flag[:, 0:1], viol, AX.X).then_inc(flag_in, 1)
                dve.wait_ge(flag_all, 1)
                v.tensor_copy(flag_i[:, :], flag[0:1, 1:2])
                dve.wait_ge(w2_mm, 1)
                v.tensor_copy(W2T[:, :, :], Z[1][:, :].rearrange("p (k d) -> p k d", k=2))
                link(v.memset(umb[:, :], 0.0))
                v.tensor_copy(umb[0:1, :], Y[1][0:1, 0:D])
                v.tensor_copy(sel[:, :], ident[0:2, 1:2])
                dve.wait_ge(tab_h, 16 * NC)
                v.memset(big[:, 0:2 * AW], 0.0)
                link(v.memset(aggC, 0.0))
                v.tensor_copy(idx[:, 0, 0, :], src[:, (GS + LEAD) * SB:(GS + LEAD + 8) * SB])
                v.tensor_copy(idx[:, 1, 0, :], src[:, (GS + LEAD + 8) * SB:(GS + LEAD + 16) * SB])
                dve.wait_ge(ld_typ, 16)
                v.tensor_copy(idx[:, 0, 1, :], typ[:, (GS + LEAD) * SB:(GS + LEAD + 8) * SB])
                link(v.tensor_copy(idx[:, 1, 1, :], typ[:, (GS + LEAD + 8) * SB:(GS + LEAD + 16) * SB]))

        gath = [sem(f"gathered{i}") for i in range(4)]
        prod, s_ready, mm_done, p_evac, tr_done, added, idx_ok, idx_put = (sem(x) for x in
            ("products", "onehots", "window_sums", "sums_copied", "sums_turned", "sums_added", "idx_used", "idx_put"))
        x_loaded, xg_free, z_full, z_free, y_full, y_free, hg_ready, at_ready = (sem(x) for x in
            ("x_loaded", "xg_free", "z_full", "z_free", "y_full", "y_free", "hg_ready", "at_ready"))
        dd_in, dd_sd, var_in, var_sd, sm_in, sm_exp, wg_ready, wT_ready, out_ready, out_stored = (sem(x) for x in
            ("dd_in", "dd_sd", "var_in", "var_sd", "sm_in", "sm_exp", "wg_ready", "wT_ready", "out_ready", "out_stored"))
        issued, turning, measured = sem("superblocks_issued"), sem("superblocks_turning"), sem("tiles_measured")
        f_own = [sem(f"vector_own{i}") for i in range(4)]
        g_idx, g_gath, g_s, g_mm, g_ev, g_tr, g_add, g_own = (sem(x) for x in
            ("g_idx", "g_gath", "g_s", "g_mm", "g_ev", "g_tr", "g_add", "g_own"))
        ZF = 4 + 4 * NE
        YF = 1 + GT + 1 + 2 + 2 * NE + 2

        POS = ["A", "B0", "B1", "C", "D"] + [f"s{i}" for i in range(NE + 2)] + ["E"]
        assert len(POS) == GS

        def jn(J, d):
            return J + d

        def wait(eng, s, J, v):
            if isinstance(v, int) and v <= 0:
                return
            eng.wait_ge(s, v)

        def fill_no(J, j, d=0):
            if isinstance(J, int):
                return 128 * ((J + d) // 4 + 1)
            return (J - j) * 32 + 128 * ((j + d) // 4 + 1)

        def sb_pool(pool, J, j, cols):
            wait(pool, mm_done, J, J - 3)
            wait(pool, prod, J, J - 1)
            pool.sem_inc(issued, 1)
            for b in range(SB):
                for tab, dst_, ix in ((rtab, R[:, j % 2, b * DX:(b + 1) * DX], cols(1, b)),
                                      (htab, H[:, j % 4, b * DX:(b + 1) * DX], cols(0, b))):
                    pool.indirect_dma_start(out=dst_, out_offset=None, in_=tab,
                                            in_offset=bass.IndirectOffsetOnAxis(ap=ix, axis=0)).then_inc(gath[j % 4], 16)

        def sb_product(dve, J, j):
            dve.wait_ge(gath[j % 4], fill_no(J, j))
            nc.vector.tensor_tensor(H[:, j % 4, :], H[:, j % 4, :], R[:, j % 2, :], ALU.mult).then_inc(prod, 1)
            wait(dve, mm_done, J, J - 1)
            nc.vector.tensor_tensor(
                S[:, j % 2, :, :], dloc[:, ds(J * SB, SB)].unsqueeze(2).to_broadcast([P, SB, W]),
                iota_w[:, :].unsqueeze(1).to_broadcast([P, SB, W]), ALU.is_equal).then_inc(s_ready, 1)

        def sb_add(dve, J, j):
            if isinstance(J, int) and J < 0:
                return
            at = dve.value_load(base_i[0:1, ds(J, 1)], min_val=0, max_val=NP - 1)
            wait(dve, added, J, J)
            dve.wait_ge(tr_done, J + 1)
            w_ = aggT[:, :, ds(at, W)]
            nc.vector.tensor_tensor(w_, w_, PT[j % 2][:, 0:2 * W].rearrange("p (k w) -> p k w", k=2), ALU.add)
            c_ = aggC[:, ds(at, W)]
            nc.vector.tensor_tensor(c_, c_, PT[j % 2][0:2, 2 * W:3 * W], ALU.add).then_inc(added, 1)

        def sb_dve(dve, J, j, more=True):
            if more:
                sb_product(dve, J + 1, j + 1)
            sb_add(dve, J - 2, j - 2)

        def sb_turn(pe, J, j):
            if isinstance(J, int) and J < 0:
                return
            pe.wait_ge(p_evac, J + 1)
            wait(pe, added, J, J - 1)
            pe.sem_inc(turning, 1)
            for k, (lo, hi) in enumerate(((0, P), (P, D), (D, D + 2))):
                last = pe.transpose(PT[j % 2][0:hi - lo, k * W:(k + 1) * W], Psb[:, j % 2, lo:hi], ident[0:W, 0:W])
            last.then_inc(tr_done, 1)

        def sb_pe(pe, J, j):
            pe.wait_ge(s_ready, J + 1)
            wait(pe, p_evac, J, J - 1)
            for b in range(SB):
                last = pe.matmul(PA[j % 2][0:W, 0:D + 2], S[:, j % 2, b, :], H[:, j % 4, b * DX:b * DX + D + 2],
                                 start=b == 0, stop=b == SB - 1)
            last.then_inc(mm_done, 1)
            sb_turn(pe, J - 1, j - 1)

        def sb_act(act, J, j):
            act.wait_ge(mm_done, J + 1)
            wait(act, tr_done, J, J - 1)
            nc.scalar.activation(Psb[:, j % 2, 0:D + 2], PA[j % 2][0:W, 0:D + 2], ACT.Copy).then_inc(p_evac, 1)

        def none(pos):
            pass

        def grp_sp(sp, g, nt, nxt):
            if nxt:
                sp.wait_ge(xg_free, g + 1)
                load_x(sp, g + 1, nxt)
            sp.wait_ge(out_ready, g + 1)
            if isinstance(g, int) and nt < GT:
                rows = n - g * T
                sp.dma_start(out[g * T:n, :], acc[0:rows, 0, :]).then_inc(out_stored, 16)
            else:
                sp.dma_start(out[ds(g * T, T), :].rearrange("(t p) d -> p t d", p=P), acc[:, :, :]).then_inc(out_stored, 16)

        def load_x(sp, g, nt):
            sp.dma_start(xg[:, 0:nt, :], a["x"][ds(g * T, nt * P), :].rearrange("(t p) d -> p t d", p=P)).then_inc(x_loaded, 16)

        class Fill:
            def __init__(self, g, per):
                self.base, self.n = g * per, 0

            def take(self):
                self.n += 1
                return (self.n - 1) % 2, self.base + self.n

        def grp_pe(pe, g, nt, hook):
            z, y = Fill(g, ZF), Fill(g, YF)
            N = nt * P

            def turn(count):
                pe.wait_ge(hg_ready, g * 2 + count)
                for k in range(2):
                    i, no = z.take()
                    pe.wait_ge(z_free, no)
                    for t in range(nt):
                        last = pe.transpose(Z[i][:, t * P:(t + 1) * P], hg[:, t, k * P:(k + 1) * P], ident[:, :])
                    last.then_inc(z_full, 1)
                return no

            zno = turn(1)
            hook("A")
            pe.wait_ge(at_ready, g + 1)
            i, no = y.take()
            pe.wait_ge(y_free, no)
            for t in range(nt):
                last = pe.matmul(Y[i][:, t:t + 1], aC[:, t * P:(t + 1) * P], sel[:, :], start=True, stop=True)
            last.then_inc(y_full, 1)
            hook("B0")
            pe.wait_ge(z_free, zno + 2)
            for t in range(nt):
                i, no = y.take()
                pe.wait_ge(y_free, no)
                c = slice(t * P, (t + 1) * P)
                pe.matmul(Y[i][:, 0:D], hT[:, 0, c], UT[:, 0, :], start=True, stop=False)
                pe.matmul(Y[i][:, 0:D], hT[:, 1, c], UT[:, 1, :], start=False, stop=False)
                pe.matmul(Y[i][:, 0:D], ones, ub, start=False, stop=True)
                pe.matmul(Y[i][:, D:2 * D], aT[:, 0, c], W2T[:, 0, :], start=True, stop=False)
                pe.matmul(Y[i][:, D:2 * D], aT[:, 1, c], W2T[:, 1, :], start=False, stop=False)
                pe.matmul(Y[i][:, D:2 * D], aC[:, c], umb[:, :], start=False, stop=True).then_inc(y_full, 1)
            hook("B1")
            zno = turn(2)
            hook("C")
            pe.wait_ge(z_free, zno + 2)
            i, no = y.take()
            pe.wait_ge(y_free, no)
            for t in range(nt):
                c = slice(t * P, (t + 1) * P)
                o = Y[i][:, t * NE:(t + 1) * NE]
                pe.matmul(o, hT[:, 0, c], wr[:, 0, :], start=True, stop=False)
                pe.matmul(o, hT[:, 1, c], wr[:, 1, :], start=False, stop=False)
                last = pe.matmul(o, ones, br, start=False, stop=True)
            last.then_inc(y_full, 1)
            hook("D")
            done1, done2 = {}, {}

            def layer(wt, x, e_, done, need):
                for m in range(2):
                    i, no = z.take()
                    pe.wait_ge(z_free, no)
                    if need is not None and m == 0:
                        pe.wait_ge(z_free, need + 2)
                    for k in range(2):
                        last = pe.matmul(Z[i][:, 0:N], wt[:, e_, k, m * P:(m + 1) * P], x[:, k, 0:N], start=k == 0, stop=k == 1)
                    last.then_inc(z_full, 1)
                    done[e_] = no

            for s in range(NE + 2):
                if s == 2:
                    pe.wait_ge(wg_ready, g + 1)
                    for hf in range((nt + 1) // 2):
                        i, no = y.take()
                        pe.wait_ge(y_free, no)
                        for t in range(2 * hf, min(nt, 2 * hf + 2)):
                            last = pe.transpose(Y[i][0:NE, (t % 2) * P:(t % 2 + 1) * P], wg[:, t, :], ident[:, :])
                        last.then_inc(y_full, 1)
                if s < NE:
                    layer(w1, hT, s, done1, None)
                if 0 < s <= NE:
                    layer(w2, h1[:, (s - 1) % 2, :, :], s - 1, done2, done1[s - 1])
                if s > 1:
                    e_ = s - 2
                    pe.wait_ge(z_free, done2[e_] + 2)
                    for hf in range((nt + 1) // 2):
                        i, no = y.take()
                        pe.wait_ge(y_free, no)
                        for t in range(2 * hf, min(nt, 2 * hf + 2)):
                            for k in range(2):
                                last = pe.matmul(Y[i][:, (t % 2) * D:(t % 2 + 1) * D], h2[:, e_ % 2, k, t * P:(t + 1) * P],
                                                 wo[:, e_, k, :], start=k == 0, stop=k == 1)
                        last.then_inc(y_full, 1)
                hook(f"s{s}")
            pe.wait_ge(wT_ready, g + 1)
            for hf in range((nt + 1) // 2):
                i, no = y.take()
                pe.wait_ge(y_free, no)
                for t in range(2 * hf, min(nt, 2 * hf + 2)):
                    last = pe.matmul(Y[i][:, (t % 2) * D:(t % 2 + 1) * D], wT[:, t * P:(t + 1) * P], bo, start=True, stop=True)
                last.then_inc(y_full, 1)
            hook("E")
            assert nt < GT or (z.n, y.n) == (ZF, YF), (z.n, y.n)

        def grp_act(act, g, nt, hook, agg_wait):
            z = Fill(g, ZF)
            N = nt * P
            s_ = nc.scalar

            def drain(dst_, f):
                i, no = z.take()
                act.wait_ge(z_full, no)
                f(dst_, Z[i][:, 0:N]).then_inc(z_free, 1)

            def copy(o, i_):
                return s_.activation(o, i_, ACT.Copy)

            act.wait_ge(*agg_wait)
            copy(aT[:, :, 0:N], aggT[:, :, ds(g * T, N)])
            copy(aC[:, 0:N], aggC[:, ds(g * T, N)]).then_inc(at_ready, 1)
            for k in range(2):
                drain(hT[:, k, 0:N], copy)
            hook("A")
            hook("B0")
            act.wait_ge(dd_in, g + 1)
            s_.activation(dd[:, 0:nt], dd[:, 0:nt], ACT.Sqrt).then_inc(dd_sd, 1)
            hook("B1")
            act.wait_ge(var_in, g + 1)
            s_.activation(rs[:, 0:nt], rs[:, 0:nt], ACT.Sqrt).then_inc(var_sd, 1)
            for k in range(2):
                drain(hT[:, k, 0:N], copy)
            hook("C")
            act.wait_ge(sm_in, g + 1)
            s_.activation(wg[:, 0:nt, :], wg[:, 0:nt, :], ACT.Exp).then_inc(sm_exp, 1)
            hook("D")

            def layer(l, e_, o):
                for m in range(2):
                    c = e_ * 2 + m
                    drain(o[:, m, 0:N], lambda d_, i_: s_.activation(
                        d_, i_, ACT.Relu, bias=bns[:, l, 1, c:c + 1], scale=bns[:, l, 0, c:c + 1]))

            for s in range(NE + 2):
                if s < NE:
                    layer(0, s, h1[:, s % 2, :, :])
                if 0 < s <= NE:
                    layer(1, s - 1, h2[:, (s - 1) % 2, :, :])
                hook(f"s{s}")
            hook("E")

        def grp_dve(dve, g, nt, hook, own, g0, per):
            y = Fill(g, YF)
            v = nc.vector
            count = [0]
            base = (g - g0) * per

            def mark(ins):
                count[0] += 1
                ins.then_inc(own, 1)
                return count[0]

            def since(c):
                dve.wait_ge(own, base + c)

            def link(ins):
                since(mark(ins))

            def full():
                i, no = y.take()
                dve.wait_ge(y_full, no)
                return Y[i]

            v.tensor_copy(gm[:, 0, 0:nt], mean[:, ds(g * GT, nt)])
            link(v.tensor_copy(gm[:, 1, 0:nt], rstd[:, ds(g * GT, nt)]))
            dve.wait_ge(x_loaded, g * 16 + 16)
            for t in range(nt):
                last = v.tensor_scalar(hg[:, t, :], xg[:, t, :], gm[:, 0, t:t + 1], gm[:, 1, t:t + 1], ALU.add, ALU.mult)
            last.then_inc(hg_ready, 1)
            hook("A")
            b = full()
            v.tensor_scalar(dd[:, 0:nt], b[:, 0:nt], 1.0, None, ALU.max).then_inc(dd_in, 1)
            dve.wait_ge(dd_in, g + 1)
            dve.sem_inc(y_free, 1)
            hook("B0")
            dve.wait_ge(dd_sd, g + 1)
            link(v.reciprocal(dd[:, 0:nt], dd[:, 0:nt]))
            dve.wait_ge(out_stored, g * 16 + 16)
            marks = {}
            for t in range(nt):
                b = full()
                link(v.scalar_tensor_tensor(out=acc[:, t, :], in0=b[:, D:2 * D], scalar=dd[:, t:t + 1], in1=xg[:, t, :],
                                            op0=ALU.mult, op1=ALU.add))
                v.tensor_tensor(acc[:, t, :], acc[:, t, :], b[:, 0:D], ALU.add).then_inc(y_free, 1)
            v.sem_inc(xg_free, 1)
            dve.wait_ge(y_free, y.base + y.n + 2)
            for t in range(nt):
                m_ = mark(v.bn_stats(st[:, t, :], acc[:, t, :]))
            since(m_)
            dve.sem_inc(measured, 1)
            for t in range(nt):
                m_ = mark(v.bn_aggr(mv[:, t, :], st[:, t, :]))
            since(m_)
            v.tensor_scalar(rs[:, 0:nt], mv[:, 0:nt, 1:2].rearrange("p t o -> p (t o)"), LN_EPS, None, ALU.add).then_inc(var_in, 1)
            hook("B1")
            dve.wait_ge(var_sd, g + 1)
            link(v.reciprocal(rs[:, 0:nt], rs[:, 0:nt]))
            for t in range(nt):
                last = v.tensor_scalar(hg[:, t, :], acc[:, t, :], mv[:, t, 0:1], rs[:, t:t + 1], ALU.subtract, ALU.mult)
            last.then_inc(hg_ready, 1)
            hook("C")
            b = full()
            lg = b[:, 0:nt * NE].rearrange("p (t e) -> p t e", e=NE)
            link(v.reduce_max(mx[:, 0:nt], lg, AX.X))
            link(v.tensor_tensor(wg[:, 0:nt, :], lg, mx[:, 0:nt].unsqueeze(2).to_broadcast([P, nt, NE]), ALU.subtract))
            dve.sem_inc(sm_in, 1)
            dve.sem_inc(y_free, 1)
            hook("D")
            dve.wait_ge(sm_exp, g + 1)
            link(v.reduce_sum(mx[:, 0:nt], wg[:, 0:nt, :], AX.X))
            link(v.reciprocal(mx[:, 0:nt], mx[:, 0:nt]))
            v.tensor_tensor(wg[:, 0:nt, :], wg[:, 0:nt, :], mx[:, 0:nt].unsqueeze(2).to_broadcast([P, nt, NE]),
                            ALU.mult).then_inc(wg_ready, 1)
            dve.wait_ge(wg_ready, g + 1)
            m_acc = {}
            for s in range(NE + 2):
                if s == 2:
                    for hf in range((nt + 1) // 2):
                        b = full()
                        w_ = min(nt - 2 * hf, 2) * P
                        last = v.tensor_copy(wT[:, hf * 2 * P:hf * 2 * P + w_], b[0:NE, 0:w_])
                        last.then_inc(y_free, 1)
                    dve.wait_ge(y_free, y.base + y.n + 2)
                    dve.sem_inc(wT_ready, 1)
                if s > 1:
                    e_ = s - 2
                    for hf in range((nt + 1) // 2):
                        b = full()
                        if hf in m_acc:
                            since(m_acc[hf])
                        for t in range(2 * hf, min(nt, 2 * hf + 2)):
                            last = v.scalar_tensor_tensor(out=acc[:, t, :], in0=b[:, (t % 2) * D:(t % 2 + 1) * D],
                                                          scalar=wg[:, t, e_:e_ + 1], in1=acc[:, t, :],
                                                          op0=ALU.mult, op1=ALU.add)
                            if t < min(nt, 2 * hf + 2) - 1:
                                continue
                            m_acc[hf] = mark(last)
                        since(m_acc[hf])
                        dve.sem_inc(y_free, 1)
                hook(f"s{s}")
            for hf in range((nt + 1) // 2):
                b = full()
                w_ = min(nt - 2 * hf, 2) * D
                o = acc[:, 2 * hf:min(nt, 2 * hf + 2), :].rearrange("p t d -> p (t d)")
                v.tensor_tensor(o, o, b[:, 0:w_], ALU.add).then_inc(y_free, 1)
            dve.wait_ge(y_free, y.base + y.n + 2)
            dve.sem_inc(out_ready, 1)
            hook("E")
            assert nt < GT or count[0] == per, count[0]

        PER = 1 + 1 + GT + 2 * GT + 1 + 4 + 2 * NE

        def groups(emit):
            def run(eng):
                with eng.Fori(0, NG - 2) as g:
                    emit(eng, g, GT, GT, 2, 0)
                emit(eng, NG - 2, GT, 1, 3, NG - 2)
                emit(eng, NG - 1, 1, 0, 3, NG - 2)
            return run

        LAST = NSB * NW

        def branches(eng, fast, general):
            broken = eng.value_load(flag_i[0:1, 0:1], min_val=-NP, max_val=NP)
            with eng.If(broken > 0):
                general()
            with eng.Else():
                fast()

        with nc.Block() as block:
            @block.sync
            def _(sp):
                load_x(sp, 0, GT)
                sp.sem_inc(out_stored, 16)
                with sp.Fori(0, NG - 2) as g:
                    grp_sp(sp, g, GT, GT)
                grp_sp(sp, NG - 2, GT, 1)
                grp_sp(sp, NG - 1, 1, 0)
                sp.wait_ge(out_stored, 16 * NG + 16)

            @block.gpsimd
            def _(pool):
                def fast():
                    for J in range(GS + LEAD):
                        sb_pool(pool, J, J, lambda s, b: (src, typ)[s][:, J * SB + b:J * SB + b + 1])
                    with pool.Fori(1, NG - 1) as k:
                        for j in range(GS):
                            if j % 8 == 0:
                                if j == 0:
                                    pool.wait_ge(idx_put, k * 2 - 1)
                                else:
                                    pool.wait_ge(idx_put, k * 2)
                            sb_pool(pool, k * GS + (LEAD + j), j, lambda s, b: idx[:, j // 8, s, (j % 8) * SB + b:(j % 8) * SB + b + 1])

                def general():
                    with pool.Fori(0, NSB) as J:
                        pool.wait_ge(g_idx, J + 1)
                        pool.sem_inc(issued, 1)
                        for b in range(SB):
                            for tab, dst_, s in ((rtab, R, 1), (htab, H, 0)):
                                pool.indirect_dma_start(
                                    out=dst_[:, 0, b * DX:(b + 1) * DX], out_offset=None, in_=tab,
                                    in_offset=bass.IndirectOffsetOnAxis(ap=idx[:, 0, s, b:b + 1], axis=0)).then_inc(g_gath, 16)

                branches(pool, fast, general)

            @block.scalar
            def _(act):
                def fast():
                    for J in range(GS + LEAD):
                        sb_act(act, J, J)
                    with act.Fori(1, NG - 1) as k:
                        hook = lambda p: sb_act(act, k * GS + (LEAD + POS.index(p)), POS.index(p))
                        grp_act(act, k - 1, GT, hook, (added, k * GS + (LEAD - 2)))
                    grp_act(act, NG - 2, GT, none, (added, NSB))
                    grp_act(act, NG - 1, 1, none, (added, NSB))

                def general():
                    with act.Fori(0, NSB) as J:
                        with act.Fori(0, NW) as w:
                            act.wait_ge(g_mm, J * NW + w + 1)
                            nc.scalar.activation(Psb[:, 0, 0:D + 2], PA[0][0:W, 0:D + 2], ACT.Copy).then_inc(g_ev, 1)
                    groups(lambda eng, g, nt, nx, r, g0: grp_act(eng, g, nt, none, (g_add, LAST)))(act)

                branches(act, fast, general)

            @block.tensor
            def _(pe):
                def fast():
                    for J in range(GS + LEAD):
                        sb_pe(pe, J, J)
                    with pe.Fori(1, NG - 1) as k:
                        hook = lambda p: sb_pe(pe, k * GS + (LEAD + POS.index(p)), POS.index(p))
                        grp_pe(pe, k - 1, GT, hook)
                    sb_turn(pe, NSB - 1, NSB - 1)
                    grp_pe(pe, NG - 2, GT, none)
                    grp_pe(pe, NG - 1, 1, none)

                def general():
                    with pe.Fori(0, NSB) as J:
                        with pe.Fori(0, NW) as w:
                            pe.wait_ge(g_s, J * NW + w + 1)
                            for b in range(SB):
                                last = pe.matmul(PA[0][0:W, 0:D + 2], S[:, 0, b, :], H[:, 0, b * DX:b * DX + D + 2],
                                                 start=b == 0, stop=b == SB - 1)
                            last.then_inc(g_mm, 1)
                            pe.wait_ge(g_ev, J * NW + w + 1)
                            pe.sem_inc(turning, 1)
                            for k, (lo, hi) in enumerate(((0, P), (P, D), (D, D + 2))):
                                last = pe.transpose(PT[0][0:hi - lo, k * W:(k + 1) * W], Psb[:, 0, lo:hi], ident[0:W, 0:W])
                            last.then_inc(g_tr, 1)
                    groups(lambda eng, g, nt, nx, r, g0: grp_pe(eng, g, nt, none))(pe)

                branches(pe, fast, general)

            @block.vector
            def _(dve):
                v = nc.vector
                dve.sem_inc(z_free, 2)
                dve.sem_inc(y_free, 2)

                def fast():
                    sb_product(dve, 0, 0)
                    for J in range(GS + LEAD):
                        sb_dve(dve, J, J, J < GS + LEAD - 1)
                    dve.sem_inc(idx_put, 2)
                    with dve.Fori(1, NG - 1) as k:
                        def hook(p):
                            j = POS.index(p)
                            J = k * GS + (LEAD + j)
                            if j < GS - 1:
                                sb_dve(dve, J, j)
                            else:
                                tail(J, j)
                            if j % 8 == 6 or j == GS - 1:
                                pass
                            if j == 7 or j == GS - 1:
                                hf = j // 8
                                for s, t in enumerate((src, typ)):
                                    last = v.tensor_copy(idx[:, hf, s, :], t[:, ds((k * GS + (LEAD + GS + 8 * hf)) * SB, 8 * SB)])
                                last.then_inc(idx_put, 1)

                        def tail(J, j):
                            sb_add(dve, J - 2, j - 2)

                        sb_product(dve, k * GS + LEAD, 0)
                        grp_dve(dve, k - 1, GT, hook, f_own[0], 0, PER)
                    sb_add(dve, NSB - 2, NSB - 2)
                    sb_add(dve, NSB - 1, NSB - 1)
                    grp_dve(dve, NG - 2, GT, none, f_own[1], NG - 2, PER)
                    grp_dve(dve, NG - 1, 1, none, f_own[1], NG - 2, PER)

                def general():
                    own = [0]

                    def link(ins):
                        own[0] += 1
                        ins.then_inc(f_own[3], 1)
                        dve.wait_ge(f_own[3], own[0])

                    dl = dloc[:, :].rearrange("p (s b) -> p s b", b=SB)
                    link(v.tensor_tensor(dl, dl, Z[0][:, 0:NSB].unsqueeze(2).to_broadcast([P, NSB, SB]), ALU.add))
                    with dve.Fori(0, NSB) as J:
                        for s, t in enumerate((src, typ)):
                            last = v.tensor_copy(idx[:, 0, s, 0:SB], t[:, ds(J * SB, SB)])
                        last.then_inc(g_idx, 1)
                        dve.wait_ge(g_gath, J * 128 + 128)
                        v.tensor_tensor(H[:, 0, :], H[:, 0, :], R[:, 0, :], ALU.mult)
                        v.tensor_copy(dwin[:, :], dloc[:, ds(J * SB, SB)]).then_inc(f_own[2], 1)
                        with dve.Fori(0, NW) as w:
                            dve.wait_ge(f_own[2], J * (NW + 1) + w + 1)
                            v.tensor_tensor(S[:, 0, :, :], dwin[:, :].unsqueeze(2).to_broadcast([P, SB, W]),
                                            iota_w[:, :].unsqueeze(1).to_broadcast([P, SB, W]), ALU.is_equal).then_inc(g_s, 1)
                            dve.wait_ge(g_s, J * NW + w + 1)
                            v.tensor_scalar(dwin[:, :], dwin[:, :], float(-W), None, ALU.add).then_inc(f_own[2], 1)
                            dve.wait_ge(g_tr, J * NW + w + 1)
                            w_ = aggT[:, :, ds(w * W, W)]
                            v.tensor_tensor(w_, w_, PT[0][:, 0:2 * W].rearrange("p (k w) -> p k w", k=2), ALU.add)
                            c_ = aggC[:, ds(w * W, W)]
                            v.tensor_tensor(c_, c_, PT[0][0:2, 2 * W:3 * W], ALU.add).then_inc(g_add, 1)
                            dve.wait_ge(g_add, J * NW + w + 1)
                    groups(lambda eng, g, nt, nx, r, g0: grp_dve(eng, g, nt, none, (f_own[0] if r == 2 else f_own[1]), g0, PER))(dve)

                branches(dve, fast, general)


def layout(x, src, dst, edge_type_500, L0_gnn_relation_emb, L0_gnn_msg_w, L0_gnn_msg_b, L0_gnn_upd_w,
           L0_gnn_upd_b, L0_gnn_gate_w, L0_gnn_gate_b, **f):
    n, e, nrel = x.shape[0], src.shape[0], L0_gnn_relation_emb.shape[0]
    nt, ng, nsb = sizes(n, e)
    nb = nsb * SB

    def cols(v, fill, wide):
        v = np.asarray(v)
        o = np.full(wide * P, fill, v.dtype)
        o[:e] = v
        return np.ascontiguousarray(o.reshape(wide, P).T)

    dst = np.asarray(dst)
    wide = nb + GS * SB
    x = np.asarray(x)
    xp = np.zeros((nt * P, D), x.dtype)
    xp[:n] = x
    at = ((0, 1, 2, 3), (1, 0, 3, 2), (2, 3, 0, 1), (3, 2, 1, 0))
    mw, uw = np.asarray(L0_gnn_msg_w), np.asarray(L0_gnn_upd_w)
    km = np.concatenate([np.concatenate([mw[i] for i in row], 1) for row in at], 0)
    u = np.concatenate([np.concatenate([uw[i] for i in row], 1) for row in at], 0)
    ut = u.T.reshape(D, 4, 64).transpose(0, 2, 1).reshape(D, D)
    g = {k[len("L0_ffn_"):]: np.asarray(v) for k, v in f.items()}
    bn = np.stack([np.stack([g[k + str(l)].reshape(NE * 2, P).T for k in ("b", "g", "be", "m", "v")], 1) for l in (1, 2)], 1)
    return {
        "x": xp, "src": cols(src, n, wide), "typ": cols(edge_type_500, nrel, wide), "dst": cols(dst, dst[-1], nb),
        "rel": np.asarray(L0_gnn_relation_emb),
        "gw": np.asarray(L0_gnn_gate_w).reshape(64, 4).T.reshape(D), "gb": np.asarray(L0_gnn_gate_b),
        "km": km, "ut": ut, "mb": np.asarray(L0_gnn_msg_b).reshape(2, P).T,
        "ub": np.asarray(L0_gnn_upd_b).T.reshape(1, D),
        "bn": bn, "wr": g["Wr"], "br": g["br"].reshape(1, NE), "bo": g["bo"],
        "w1": g["W1"], "w2": g["W2"], "wo": g["Wo"],
    }, n, e, nrel


def kernel(**inputs):
    import concourse.bacc as bacc
    from concourse.bass_utils import run_bass_kernel_spmd

    data, n, e, nrel = layout(**inputs)
    nc = bacc.Bacc("TRN2", target_bir_lowering=False, num_devices=1)
    arrays = {f"in_{k}": np.ascontiguousarray(v) for k, v in data.items()}
    aps = {k[3:]: nc.dram_tensor(k, v.shape, mybir.dt.from_np(v.dtype), kind="ExternalInput").ap() for k, v in arrays.items()}
    out = nc.dram_tensor("out", (n, D), mybir.dt.float32, kind="ExternalOutput").ap()
    build(nc, aps, out, n, e, nrel)
    r = run_bass_kernel_spmd(nc, [arrays], core_ids=[0])
    return r.results[0]["out"]
```

```python
from contextlib import ExitStack

import numpy as np
import concourse.bass as bass
from concourse import mybir

P = 128
D = 256
DX = 260
NE = 8
W = 64
SB = 4
GT = 2
GS = 8
LEAD = 4
LN_EPS = 1e-5
BN_EPS = 1e-3
NEG = ((0, 3), (1, 2), (2, 3))


def sizes(n, e):
    nt = -(-n // P)
    ng = -(-nt // GT)
    nsb = GS * (ng - 2) + GS + LEAD
    assert nt == GT * (ng - 1) + 1 and 0 <= nsb * SB * P - e, (nt, ng, nsb, e)
    return nt, ng, nsb


def build(nc, a, out, n, e, nrel):
    fp32, f32r, i32, bf16 = mybir.dt.float32, mybir.dt.float32r, mybir.dt.int32, mybir.dt.bfloat16
    ALU, ACT, AX = mybir.AluOpType, mybir.ActivationFunctionType, mybir.AxisListType
    NT, NG, NSB = sizes(n, e)
    NB = NSB * SB
    NBI = NB + GS * SB
    NP = NT * P
    RT = nrel // 4
    T = GT * P
    AW = 3 * T
    NW = T // W
    HB = max(h for h in range(1, 17) if NB % (2 * h) == 0)
    ds = bass.ds

    htab = nc.dram_tensor("h_table", [NP, DX], fp32, kind="Internal").ap()
    rtab = nc.dram_tensor("r_table", [nrel + 1, DX], fp32, kind="Internal").ap()

    ctx = ExitStack()
    with ctx:
        def sb(name, shape, dt=fp32):
            return ctx.enter_context(nc.sbuf_tensor(name, shape, dt))

        def sem(name):
            return ctx.enter_context(nc.semaphore(name))

        agg = sb("agg", [P, 3, AW])
        aggT = agg[:, 0:2, :]
        aggC = agg[0:2, 2, :]
        early = ExitStack()

        def sb0(name, shape, dt=fp32):
            return early.enter_context(nc.sbuf_tensor(name, shape, dt))

        w1, w2, wo = (sb(x, [P, NE, 2, D]) for x in ("w1", "w2", "wo"))
        H = sb("H", [P, 4, SB * DX])
        R = sb("R", [P, 2, SB * DX])
        src = sb("src", [P, NBI], i32)
        typ = sb("typ", [P, NBI], i32)
        idx = sb("idx", [P, 2, 2, GS * SB // 2], i32)
        dloc = sb("dloc", [P, NB + SB])
        dwin = sb("dwin", [P, SB])
        S = sb("S", [P, 2, SB, W], f32r)
        Psb = sb("Psb", [W, 2, DX])
        xg = sb("xg", [P, GT, D])
        acc = sb("acc", [P, GT, D])
        hg = sb("hg", [P, GT, D])
        hT = sb("hT", [P, 2, T])
        aT = sb("aT", [P, 2, T])
        aC = sb("aC", [2, T])
        h1 = sb("h1", [P, 2, 2, T])
        h2 = sb("h2", [P, 2, 2, T])
        UT = sb("UT", [P, 2, D])
        W2T = sb("W2T", [P, 2, D])
        umb = sb("umb", [2, D])
        ub_all = sb("ub_all", [P, D])
        br_all = sb("br_all", [P, NE])
        wr = sb("wr", [P, 2, NE])
        few = sb("few", [P, D + T])
        bo = few[32:32 + NE, 0:D]
        wT = few[32:32 + NE, D:D + T]
        base_i = few[96:97, 0:NSB].bitcast(i32)
        bns = sb("bns", [P, 2, 2, NE * 2])
        ident = sb("ident", [P, P])
        iota_w = sb("iota_w", [P, W])
        sel = sb("sel", [2, 1])
        mean = sb("mean", [P, NT + GT])
        rstd = sb("rstd", [P, NT + GT])
        flag = sb("flag", [P, 4])
        flag_i = sb("flag_i", [1, 1], i32)
        gm = sb("gm", [P, 2, GT])
        dd = sb("dd", [P, GT])
        st = sb("st", [P, GT, 6])
        mv = sb("mv", [P, GT, 2])
        rs = sb("rs", [P, GT])
        mx = sb("mx", [P, GT])
        wg = sb("wg", [P, GT, NE])
        xall = sb0("xall", [P, NT, DX])
        scratch = sb0("scratch", [P, HB * (2 * P + P // 2)])
        small = sb0("small", [P, P + 2 * NT])
        words = HB * P // 2
        oh_lo = [scratch[:, i * words:(i + 1) * words].bitcast(bf16)
                 .rearrange("p (c b) -> p c b", b=HB) for i in range(2)]
        oh_hi = [scratch[:, (3 + i) * words:(4 + i) * words].bitcast(bf16)[:, 0:HB * NT]
                 .rearrange("p (c b) -> p c b", b=HB) for i in range(2)]
        hflat = H[:, :, :].rearrange("p a b -> p (a b)")
        lo_b = hflat[:, 0:NB // 2].bitcast(bf16)
        hi_b = hflat[:, NB:NB + NB // 2].bitcast(bf16)
        lo_i = hflat[:, 2 * NB:3 * NB].bitcast(i32)
        hi_i = hflat[:, 3 * NB:4 * NB].bitcast(i32)
        rflat = R[:, :, :].rearrange("p a b -> p (a b)")
        rext = rflat[:, 0:4 * DX].rearrange("p (k c) -> p k c", k=4)
        dst_i = rflat[:, 4 * DX:4 * DX + NB].bitcast(i32)
        col = acc[0:1, 1, 0:NSB]
        rel = h1[:, :, :, :].rearrange("p a b c -> p (a b c)").rearrange("p (k c) -> p k c", k=4)
        bn = h2[:, 1, 0, 0:10 * NE * 2].rearrange("p (l q c) -> p l q c", l=2, q=5)
        ones0 = h2[0:1, 1, 1, 0:P]
        gwb = hg[:, 0, :]
        rprod = hg[:, 1, :]
        zrow = hT[0:1, :, :].rearrange("p a b -> p (a b)")[:, 0:DX]
        km = aT
        mb = acc[:, 0, 0:2]
        gbc = acc[:, 0, 2:3]
        gate = acc[:, 0, 4:8]
        egate = acc[:, 0, 8:12]
        iota_cb = scratch[:, 2 * words:3 * words].bitcast(bf16).rearrange("p (c b) -> p c b", b=HB)
        iota_f = small[:, 0:P]
        sq = xg[:, 0, :]
        ssum = small[:, P:P + NT]
        ssq = small[:, P + NT:]
        dsr = acc[:, 1, 0:NT]
        hsc = acc[:, 1, 64:64 + NT]
        hbi = acc[:, 1, 128:128 + NT]

        def bank(name):
            return ctx.enter_context(nc.psum_tensor(name, [P, 512], fp32))

        Z = [bank(f"z{i}") for i in range(4)]
        Y = [bank("y0"), bank("y1")]
        PA = bank("pa")
        PT = bank("pt")

        ld_idx, ld_dst, ld_rel, ld_cl, ld_bn, ld_ffn = (sem(x) for x in
            ("ld_idx", "ld_dst", "ld_rel", "ld_clifford", "ld_bn", "ld_experts"))
        ld_x = sem("ld_x")
        ld_typ = sem("ld_typ")
        consts, iotas = sem("consts"), sem("iotas")
        bins, oh_lo_done, oh_hi_done, oh_used, deg_done = (sem(x) for x in
            ("bins", "oh_lo_done", "oh_hi_done", "oh_used", "deg_done"))
        stats, ln_var, ln_sd, hscaled, tab_h, tab_r, r_ready, z_ready = (sem(x) for x in
            ("stats", "ln_var", "ln_sd", "hscaled", "tab_h", "tab_r", "r_ready", "z_ready"))
        gsum, gexp, cl_ready, w2_mm, base_mm, base_row, bn_in, bn_sd, ds_in, ds_sd = (sem(x) for x in
            ("gate_sum", "gate_exp", "clifford_ready", "w2_mm", "base_mm", "base_row",
             "bn_in", "bn_sd", "ds_in", "ds_sd"))
        z_dve, flag_in, flag_all, flag_done, tabs = (sem(x) for x in
            ("startup_dve", "flag_in", "flag_all", "flag_done", "tables"))
        act_own, pool_own, z_row = sem("startup_act"), sem("startup_pool"), sem("zero_row")
        HIT = NB // (2 * HB)
        assert HIT * 2 * HB == NB
        XC = 7
        NC = NT // XC if NT % XC == 0 else 1
        XN = NT // NC

        with nc.Block() as block:
            @block.sync
            def _(sp):
                sp.dma_start(src[:, :], a["src"]).then_inc(ld_idx, 16)
                sp.dma_start(dst_i, a["dst"]).then_inc(ld_dst, 16)
                sp.dma_start(rel[0:RT, :, :], a["rel"].rearrange("(k p) d -> p k d", k=4)).then_inc(ld_rel, 16)
                sp.dma_start(gwb[0:RT, :], a["gw"].partition_broadcast(RT)).then_inc(ld_rel, 16)
                sp.dma_start(gbc[0:RT, :], a["gb"].partition_broadcast(RT)).then_inc(ld_rel, 16)
                xv = a["x"].rearrange("(t p) d -> p t d", p=P)
                for c in range(NC):
                    sp.dma_start(xall[:, c * XN:(c + 1) * XN, 0:D], xv[:, c * XN:(c + 1) * XN, :]).then_inc(ld_x, 16)
                sp.dma_start(typ[:, :], a["typ"]).then_inc(ld_typ, 16)
                sp.dma_start(km[:, :, 0:D], a["km"].rearrange("(k p) d -> p k d", p=P)).then_inc(ld_cl, 16)
                sp.dma_start(UT[:, :, :], a["ut"].rearrange("(k p) d -> p k d", p=P)).then_inc(ld_cl, 16)
                sp.dma_start(mb, a["mb"]).then_inc(ld_cl, 16)
                sp.dma_start(ub_all[:, :], a["ub"].partition_broadcast(P)).then_inc(ld_cl, 16)
                sp.dma_start(bn[:, :, :, :], a["bn"]).then_inc(ld_bn, 16)
                sp.dma_start(wr[:, :, :], a["wr"].rearrange("(k p) d -> p k d", p=P)).then_inc(ld_ffn, 16)
                sp.dma_start(br_all[:, :], a["br"].partition_broadcast(P)).then_inc(ld_ffn, 16)
                sp.dma_start(bo, a["bo"]).then_inc(ld_ffn, 16)
                for t, name in ((w1, "w1"), (w2, "w2"), (wo, "wo")):
                    for i in range(NE):
                        sp.dma_start(t[:, i, :, :], a[name][i, :, :].rearrange("(k p) d -> p k d", p=P)).then_inc(ld_ffn, 16)
                sp.wait_ge(r_ready, 1)
                sp.dma_start(rtab[0:nrel, :].rearrange("(k p) c -> p k c", k=4), rext[0:RT, :, :]).then_inc(tab_r, 16)
                sp.wait_ge(z_row, 1)
                sp.dma_start(rtab[nrel:nrel + 1, :], zrow).then_inc(tab_r, 16)
                hv = htab.rearrange("(t p) c -> p t c", p=P)
                for c in range(NC):
                    sp.wait_ge(hscaled, c + 1)
                    sp.dma_start(hv[:, c * XN:(c + 1) * XN, :], xall[:, c * XN:(c + 1) * XN, :]).then_inc(tab_h, 16)
                sp.wait_ge(tab_r, 32)
                sp.wait_ge(tab_h, 16 * NC)
                sp.wait_ge(ld_ffn, 16 * (3 + 3 * NE))
                sp.wait_ge(ld_idx, 16)
                sp.wait_ge(ld_typ, 16)

            @block.gpsimd
            def _(pool):
                pool.iota(iota_f, pattern=[[1, P]], base=0, channel_multiplier=0,
                          allow_small_or_imprecise_dtypes=True).then_inc(iotas, 1)
                pool.iota(iota_cb, pattern=[[1, P], [0, HB]], base=0, channel_multiplier=0,
                          allow_small_or_imprecise_dtypes=True).then_inc(iotas, 1)
                pool.memset(ident[:, :], 0.0).then_inc(pool_own, 1)
                pool.wait_ge(pool_own, 1)
                pool.affine_select(out=ident[:, :], in_=ident[:, :], compare_op=ALU.not_equal, fill=1.0,
                                   base=0, pattern=[[-1, P]], channel_multiplier=1).then_inc(consts, 1)
                pool.memset(xall[:, :, D:DX], 0.0).then_inc(pool_own, 1)
                pool.wait_ge(pool_own, 2)
                pool.memset(xall[:, :, D + 1:D + 2], 1.0).then_inc(consts, 1)
                pool.wait_ge(flag_in, 1)
                pool.partition_all_reduce(flag[:, 1:2], flag[:, 0:1], P, bass.bass_isa.ReduceOp.max).then_inc(flag_all, 1)

            @block.scalar
            def _(act):
                own = [0]

                def link(ins):
                    own[0] += 1
                    ins.then_inc(act_own, 1)
                    act.wait_ge(act_own, own[0])

                act.wait_ge(gsum, 1)
                nc.scalar.activation(egate[0:RT, :], gate[0:RT, :], ACT.Exp, scale=-1.0).then_inc(gexp, 1)
                for c in range(NC):
                    act.wait_ge(ld_x, 16 * NC)
                    for t in range(c * XN, (c + 1) * XN):
                        last = nc.scalar.activation(sq, xall[:, t, 0:D], ACT.Copy, accum_out=ssum[:, t:t + 1])
                        link(last)
                act.mul(mean[:, 0:NT], ssum, -1.0 / D).then_inc(stats, 1)
                act.wait_ge(stats, 1)
                for t in range(NT):
                    link(nc.scalar.activation(sq, xall[:, t, 0:D], ACT.Square, bias=mean[:, t:t + 1],
                                              accum_out=ssq[:, t:t + 1]))
                act.sem_inc(stats, 1)
                act.wait_ge(ln_var, 1)
                nc.scalar.activation(rstd[:, 0:NT], rstd[:, 0:NT], ACT.Sqrt).then_inc(ln_sd, 1)
                act.wait_ge(ds_in, 1)
                nc.scalar.activation(dsr, dsr, ACT.Sqrt).then_inc(ds_sd, 1)
                act.wait_ge(bn_in, 1)
                nc.scalar.activation(bns[:, :, 0, :], bns[:, :, 0, :], ACT.Sqrt).then_inc(bn_sd, 1)

            @block.tensor
            def _(pe):
                pe.wait_ge(oh_lo_done, 1)
                with pe.Fori(0, HIT) as i:
                    for h in range(2):
                        pe.wait_ge(oh_lo_done, i * 2 + h + 2)
                        for b in range(HB):
                            last = pe.matmul(Y[0][:, 0:NT], oh_lo[h][:, :, b], oh_hi[h][:, :, b],
                                             start=False, stop=True, skip_group_check=True)
                        last.then_inc(oh_used, 1)
                pe.wait_ge(base_row, 1)
                pe.matmul(PA[:, 0:NSB], ones0, dloc[0:1, 0:NB:SB],
                          start=True, stop=True).then_inc(base_mm, 1)
                pe.wait_ge(cl_ready, 1)
                for m in range(2):
                    for k in range(2):
                        pe.matmul(Z[1][:, m * D:(m + 1) * D], km[:, k, m * P:(m + 1) * P], UT[:, k, :],
                                  start=k == 0, stop=k == 1)
                for k in range(2):
                    last = pe.matmul(Y[1][0:1, 0:D], mb[:, k:k + 1], UT[:, k, :], start=k == 0, stop=k == 1)
                last.then_inc(w2_mm, 1)

            @block.vector
            def _(dve):
                own = [0]

                def link(ins):
                    own[0] += 1
                    ins.then_inc(z_dve, 1)
                    dve.wait_ge(z_dve, own[0])

                v = nc.vector
                dve.wait_ge(ld_rel, 48)
                for k in range(4):
                    link(v.tensor_tensor(rprod[0:RT, :], rel[0:RT, k, :], gwb[0:RT, :], ALU.mult))
                    link(v.reduce_sum(gate[0:RT, k:k + 1], rprod[0:RT, :], AX.X))
                v.tensor_scalar(gate[0:RT, :], gate[0:RT, :], gbc[0:RT, :], None, ALU.add).then_inc(gsum, 1)
                dve.wait_ge(ld_idx, 16)
                dve.wait_ge(iotas, 2)
                v.memset(ones0, 1.0)
                v.tensor_copy(iota_w[:, :], iota_f[:, 0:W])
                v.memset(zrow, 0.0).then_inc(z_row, 1)
                v.tensor_scalar(lo_i, src[:, 0:NB], P - 1, None, ALU.bitwise_and)
                link(v.tensor_scalar(hi_i, src[:, 0:NB], 7, None, ALU.logical_shift_right))
                v.tensor_copy(lo_b, lo_i)
                v.tensor_copy(hi_b, hi_i).then_inc(bins, 1)
                v.memset(Y[0][:, 0:NT], 0.0).then_inc(oh_lo_done, 1)
                dve.sem_inc(oh_used, 2)
                dve.wait_ge(bins, 1)
                with dve.Fori(0, HIT) as i:
                    for h in range(2):
                        dve.wait_ge(oh_used, i * 2 + h + 1)
                        for oh, part, m in ((oh_hi[h], hi_b, NT), (oh_lo[h], lo_b, P)):
                            last = v.tensor_tensor(oh, iota_cb[:, 0:m, :],
                                                   part[:, ds(i * (2 * HB) + h * HB, HB)].unsqueeze(1).to_broadcast([P, m, HB]),
                                                   ALU.is_equal)
                        last.then_inc(oh_lo_done, 1)
                dve.wait_ge(stats, 2)
                link(v.tensor_scalar(rstd[:, 0:NT], ssq, 1.0 / D, LN_EPS, ALU.mult, ALU.add))
                v.tensor_copy(rstd[:, 0:NT], rstd[:, 0:NT]).then_inc(ln_var, 1)
                dve.wait_ge(oh_used, 2 + 2 * HIT)
                v.tensor_scalar(dsr, Y[0][:, 0:NT], 1.0, None, ALU.max).then_inc(ds_in, 1)
                dve.wait_ge(ld_bn, 16)
                v.tensor_scalar(bns[:, :, 0, :], bn[:, :, 4, :], BN_EPS, None, ALU.add).then_inc(bn_in, 1)
                dve.wait_ge(ds_sd, 1)
                link(v.reciprocal(dsr, dsr))
                dve.wait_ge(ln_sd, 1)
                link(v.reciprocal(rstd[:, 0:NT], rstd[:, 0:NT]))
                link(v.tensor_tensor(hsc, rstd[:, 0:NT], dsr, ALU.mult))
                v.tensor_tensor(hbi, mean[:, 0:NT], hsc, ALU.mult)
                dve.wait_ge(consts, 2)
                link(v.tensor_copy(xall[:, :, D:D + 1].rearrange("p t o -> p (t o)"), dsr))
                for t in range(NT):
                    last = v.tensor_scalar(xall[:, t, 0:D], xall[:, t, 0:D], hsc[:, t:t + 1], hbi[:, t:t + 1],
                                           ALU.mult, ALU.add)
                    if t % XN == XN - 1:
                        last.then_inc(hscaled, 1)
                dve.wait_ge(gexp, 1)
                link(v.tensor_scalar(egate[0:RT, :], egate[0:RT, :], 1.0, None, ALU.add))
                link(v.reciprocal(gate[0:RT, :], egate[0:RT, :]))
                link(v.memset(rext[0:RT, :, D:DX], 0.0))
                v.memset(rext[0:RT, :, D + 1:D + 2], 1.0)
                v.tensor_copy(rext[0:RT, :, D:D + 1].rearrange("p k o -> p (k o)"), gate[0:RT, :])
                for k in range(4):
                    last = v.tensor_scalar(rext[0:RT, k, 0:D], rel[0:RT, k, :], gate[0:RT, k:k + 1], None, ALU.mult)
                last.then_inc(r_ready, 1)
                dve.wait_ge(bn_sd, 1)
                link(v.reciprocal(bns[:, :, 0, :], bns[:, :, 0, :]))
                link(v.tensor_tensor(bns[:, :, 0, :], bns[:, :, 0, :], bn[:, :, 1, :], ALU.mult))
                link(v.tensor_tensor(bns[:, :, 1, :], bn[:, :, 0, :], bn[:, :, 3, :], ALU.subtract))
                link(v.tensor_tensor(bns[:, :, 1, :], bns[:, :, 1, :], bns[:, :, 0, :], ALU.mult))
                link(v.tensor_tensor(bns[:, :, 1, :], bns[:, :, 1, :], bn[:, :, 2, :], ALU.add))
                dve.wait_ge(ld_cl, 64)
                for b, q in NEG:
                    kb = km[(b % 2) * 64:(b % 2) * 64 + 64, b // 2, q * 64:q * 64 + 64]
                    v.tensor_scalar(kb, kb, -1.0, None, ALU.mult)
                    us = UT[(q % 2) * 64:(q % 2) * 64 + 64, q // 2, b:D:4]
                    last = v.tensor_scalar(us, us, -1.0, None, ALU.mult)
                last.then_inc(cl_ready, 1)
                dve.wait_ge(ld_dst, 16)
                v.memset(dloc[:, NB:NB + SB], 0.0)
                v.tensor_copy(dloc[:, 0:NB], dst_i).then_inc(base_row, 1)
                dve.wait_ge(base_row, 1)
                tmp = hflat[:, 0:NB]
                viol = hflat[:, NB:2 * NB]
                link(v.memset(tmp, 0.0))
                for g in range(NG - 2):
                    lo = (GS * (g + 1) + LEAD - 1) * SB
                    hi = (GS * (g + 2) + LEAD - 1) * SB if g < NG - 3 else NB
                    link(v.memset(tmp[:, lo:hi], float(T * (g + 1))))
                link(v.tensor_tensor(viol, tmp, dloc[:, 0:NB], ALU.subtract))
                link(v.tensor_scalar(col, viol[0:1, 0:NB:SB], -1.0, 0.0, ALU.mult, ALU.max))
                v.tensor_scalar(base_i, col, float(AW - W), None, ALU.min)
                link(v.tensor_scalar(tmp, viol, -1.0, float(W - AW), ALU.mult, ALU.add))
                link(v.tensor_tensor(viol, viol, tmp, ALU.max))
                dve.wait_ge(base_mm, 1)
                link(v.tensor_tensor(dloc[:, 0:NB].rearrange("p (s b) -> p s b", b=SB),
                                     dloc[:, 0:NB].rearrange("p (s b) -> p s b", b=SB),
                                     PA[:, 0:NSB].unsqueeze(2).to_broadcast([P, NSB, SB]), ALU.subtract))
                link(v.tensor_scalar(tmp, dloc[:, 0:NB], -1.0, None, ALU.mult))
                link(v.tensor_tensor(viol, viol, tmp, ALU.max))
                link(v.tensor_scalar(tmp, dloc[:, 0:NB], float(1 - W), None, ALU.add))
                link(v.tensor_tensor(viol, viol, tmp, ALU.max))
                v.reduce_max(flag[:, 0:1], viol, AX.X).then_inc(flag_in, 1)
                dve.wait_ge(flag_all, 1)
                v.tensor_copy(flag_i[:, :], flag[0:1, 1:2])
                dve.wait_ge(w2_mm, 1)
                v.tensor_copy(W2T[:, :, :], Z[1][:, :].rearrange("p (k d) -> p k d", k=2))
                link(v.memset(umb[:, :], 0.0))
                v.tensor_copy(umb[0:1, :], Y[1][0:1, 0:D])
                v.tensor_copy(sel[:, :], ident[0:2, 1:2])
                dve.wait_ge(tab_h, 16 * NC)
                v.memset(agg[:, :, :], 0.0)
                v.tensor_copy(idx[:, 0, 0, :], src[:, (GS + LEAD + 0 * GS // 2) * SB:(GS + LEAD + 1 * GS // 2) * SB])
                v.tensor_copy(idx[:, 1, 0, :], src[:, (GS + LEAD + 1 * GS // 2) * SB:(GS + LEAD + 2 * GS // 2) * SB])
                dve.wait_ge(ld_typ, 16)
                v.tensor_copy(idx[:, 0, 1, :], typ[:, (GS + LEAD + 0 * GS // 2) * SB:(GS + LEAD + 1 * GS // 2) * SB])
                link(v.tensor_copy(idx[:, 1, 1, :], typ[:, (GS + LEAD + 1 * GS // 2) * SB:(GS + LEAD + 2 * GS // 2) * SB]))

        early.close()
        Xh = sb("Xh", [P, 2, SB * DX], f32r)
        Xl = sb("Xl", [P, 2, SB * DX], f32r)
        zeros = sb("zeros", [P, 3, T])
        shifted = sem("sums_shifted")
        hi_done, lo_done = sem("products_hi"), sem("products_lo")
        gath = [sem(f"gathered{i}") for i in range(4)]
        prod, s_ready, mm_done, p_evac, tr_done, added, idx_ok, idx_put = (sem(x) for x in
            ("products", "onehots", "window_sums", "sums_copied", "sums_turned", "sums_added", "idx_used", "idx_put"))
        x_loaded, xg_free, z_full, z_free, y_full, y_free, hg_ready, at_ready = (sem(x) for x in
            ("x_loaded", "xg_free", "z_full", "z_free", "y_full", "y_free", "hg_ready", "at_ready"))
        dd_in, dd_sd, var_in, var_sd, sm_in, sm_exp, wg_ready, wT_ready, out_ready, out_stored = (sem(x) for x in
            ("dd_in", "dd_sd", "var_in", "var_sd", "sm_in", "sm_exp", "wg_ready", "wT_ready", "out_ready", "out_stored"))
        issued, turning, measured = sem("superblocks_issued"), sem("superblocks_turning"), sem("tiles_measured")
        f_own = [sem(f"vector_own{i}") for i in range(4)]
        g_idx, g_gath, g_s, g_mm, g_ev, g_tr, g_add, g_own = (sem(x) for x in
            ("g_idx", "g_gath", "g_s", "g_mm", "g_ev", "g_tr", "g_add", "g_own"))
        ZF = 4 + 4 * NE
        YF = 1 + GT + 1 + GT // 2 * (NE + 2)

        POS = ["A", "B1", "s0", "s2", "s3", "s5", "s6", "s8"]
        assert len(POS) == GS
        HG = GS // 2

        def jn(J, d):
            return J + d

        def wait(eng, s, J, v):
            if isinstance(v, int) and v <= 0:
                return
            eng.wait_ge(s, v)

        def fill_no(J, j, d=0):
            if isinstance(J, int):
                return 128 * ((J + d) // 4 + 1)
            return (J - j) * 32 + 128 * ((j + d) // 4 + 1)

        def sb_pool(pool, J, j, cols):
            wait(pool, lo_done, J, J - 3)
            wait(pool, prod, J, J - 1)
            pool.sem_inc(issued, 1)
            for b in range(SB):
                for tab, dst_, ix in ((rtab, R[:, j % 2, b * DX:(b + 1) * DX], cols(1, b)),
                                      (htab, H[:, j % 4, b * DX:(b + 1) * DX], cols(0, b))):
                    pool.indirect_dma_start(out=dst_, out_offset=None, in_=tab,
                                            in_offset=bass.IndirectOffsetOnAxis(ap=ix, axis=0)).then_inc(gath[j % 4], 16)

        def sb_product(dve, J, j):
            dve.wait_ge(gath[j % 4], fill_no(J, j))
            nc.vector.tensor_tensor(H[:, j % 4, :], H[:, j % 4, :], R[:, j % 2, :], ALU.mult).then_inc(prod, 1)
            wait(dve, mm_done, J, J - 1)
            nc.vector.tensor_tensor(
                S[:, j % 2, :, :], dloc[:, ds(J * SB, SB)].unsqueeze(2).to_broadcast([P, SB, W]),
                iota_w[:, :].unsqueeze(1).to_broadcast([P, SB, W]), ALU.is_equal).then_inc(s_ready, 1)

        def split_hi(act, J, j):
            act.wait_ge(prod, J + 1)
            wait(act, mm_done, J, J - 1)
            nc.scalar.activation(Xh[:, j % 2, :], H[:, j % 4, :], ACT.Copy).then_inc(hi_done, 1)

        def split_lo(dve, J, j):
            dve.wait_ge(hi_done, J + 1)
            nc.vector.tensor_tensor(Xl[:, j % 2, :], H[:, j % 4, :], Xh[:, j % 2, :].bitcast(fp32), ALU.subtract).then_inc(lo_done, 1)

        def sb_add(dve, J, j):
            if isinstance(J, int) and J < 0:
                return
            at = dve.value_load(base_i[0:1, ds(J, 1)], min_val=0, max_val=AW - W)
            wait(dve, added, J, J)
            dve.wait_ge(tr_done, J + 1)
            w_ = aggT[:, :, ds(at, W)]
            nc.vector.tensor_tensor(w_, w_, PT[:, 0:2 * W].rearrange("p (k w) -> p k w", k=2), ALU.add)
            c_ = aggC[:, ds(at, W)]
            nc.vector.tensor_tensor(c_, c_, PT[0:2, 2 * W:3 * W], ALU.add).then_inc(added, 1)

        def sb_dve(dve, J, j):
            sb_product(dve, J + 1, j + 1)
            sb_add(dve, J - 1, j - 1)
            split_lo(dve, J + 1, j + 1)

        def sb_turn(pe, J, j):
            if isinstance(J, int) and J < 0:
                return
            pe.wait_ge(p_evac, J + 1)
            wait(pe, added, J, J)
            pe.sem_inc(turning, 1)
            for k, (lo, hi) in enumerate(((0, P), (P, D), (D, D + 2))):
                last = pe.transpose(PT[0:hi - lo, k * W:(k + 1) * W], Psb[:, j % 2, lo:hi], ident[0:W, 0:W])
            last.then_inc(tr_done, 1)

        def sb_pe(pe, J, j):
            sb_turn(pe, J - 1, j - 1)
            pe.wait_ge(s_ready, J + 1)
            wait(pe, p_evac, J, J)
            pe.wait_ge(lo_done, J + 1)
            for b in range(SB):
                for x in (Xh, Xl):
                    last = pe.matmul(PA[0:W, 0:D + 2], S[:, j % 2, b, :], x[:, j % 2, b * DX:b * DX + D + 2],
                                     start=b == 0 and x is Xh, stop=b == SB - 1 and x is Xl)
            last.then_inc(mm_done, 1)

        def sb_act(act, J, j):
            split_hi(act, J + 1, j + 1)
            act.wait_ge(mm_done, J + 1)
            wait(act, tr_done, J, J - 1)
            nc.scalar.activation(Psb[:, j % 2, 0:D + 2], PA[0:W, 0:D + 2], ACT.Copy).then_inc(p_evac, 1)

        def none(pos):
            pass

        def grp_sp(sp, g, nt, nxt):
            if nxt:
                sp.wait_ge(xg_free, g + 1)
                load_x(sp, g + 1, nxt)
            sp.wait_ge(out_ready, g + 1)
            if isinstance(g, int) and nt < GT:
                rows = n - g * T
                sp.dma_start(out[g * T:n, :], acc[0:rows, 0, :]).then_inc(out_stored, 16)
            else:
                sp.dma_start(out[ds(g * T, T), :].rearrange("(t p) d -> p t d", p=P), acc[:, :, :]).then_inc(out_stored, 16)

        def load_x(sp, g, nt):
            sp.dma_start(xg[:, 0:nt, :], a["x"][ds(g * T, nt * P), :].rearrange("(t p) d -> p t d", p=P)).then_inc(x_loaded, 16)

        class Fill:
            def __init__(self, g, per, banks, first=0):
                assert per % banks == 0
                self.base, self.n, self.banks = g * per, first, banks

            def take(self):
                self.n += 1
                return (self.n - 1) % self.banks, self.base + self.n

        def turn(pe, z, nt, ready):
            pe.wait_ge(hg_ready, ready)
            for k in range(2):
                i, no = z.take()
                pe.wait_ge(z_free, no)
                for t in range(nt):
                    last = pe.transpose(Z[i][:, t * P:(t + 1) * P], hg[:, t, k * P:(k + 1) * P], ident[:, :])
                last.then_inc(z_full, 1)
            return no

        def grp_pe(pe, g, nt, hook, nxt):
            z, y = Fill(g, ZF, 4, 2), Fill(g, YF, 2)
            N = nt * P

            pe.wait_ge(at_ready, g + 1)
            i, no = y.take()
            pe.wait_ge(y_free, no)
            for t in range(nt):
                last = pe.matmul(Y[i][:, t:t + 1], aC[:, t * P:(t + 1) * P], sel[:, :], start=True, stop=True)
            last.then_inc(y_full, 1)
            hook("A")
            pe.wait_ge(z_free, z.base + 2 + 4)
            for t in range(nt):
                i, no = y.take()
                pe.wait_ge(y_free, no)
                c = slice(t * P, (t + 1) * P)
                pe.matmul(Y[i][:, 0:D], hT[:, 0, c], UT[:, 0, :], start=True, stop=False)
                pe.matmul(Y[i][:, 0:D], hT[:, 1, c], UT[:, 1, :], start=False, stop=True)
                pe.matmul(Y[i][:, D:2 * D], aT[:, 0, c], W2T[:, 0, :], start=True, stop=False)
                pe.matmul(Y[i][:, D:2 * D], aT[:, 1, c], W2T[:, 1, :], start=False, stop=False)
                pe.matmul(Y[i][:, D:2 * D], aC[:, c], umb[:, :], start=False, stop=True).then_inc(y_full, 1)
            hook("B1")
            zno = turn(pe, z, nt, g * 2 + 2)
            pe.wait_ge(z_free, zno + 4)
            i, no = y.take()
            pe.wait_ge(y_free, no)
            for t in range(nt):
                c = slice(t * P, (t + 1) * P)
                o = Y[i][:, t * NE:(t + 1) * NE]
                pe.matmul(o, hT[:, 0, c], wr[:, 0, :], start=True, stop=False)
                last = pe.matmul(o, hT[:, 1, c], wr[:, 1, :], start=False, stop=True)
            last.then_inc(y_full, 1)
            done1, done2 = {}, {}

            def layer(wt, x, e_, done, need):
                for m in range(2):
                    i, no = z.take()
                    pe.wait_ge(z_free, no)
                    if need is not None and m == 0:
                        pe.wait_ge(z_free, need + 4)
                    for k in range(2):
                        last = pe.matmul(Z[i][:, 0:N], wt[:, e_, k, m * P:(m + 1) * P], x[:, k, 0:N], start=k == 0, stop=k == 1)
                    last.then_inc(z_full, 1)
                    done[e_] = no

            for s in range(NE + 2):
                if s == 2:
                    pe.wait_ge(wg_ready, g + 1)
                    for hf in range((nt + 1) // 2):
                        i, no = y.take()
                        pe.wait_ge(y_free, no)
                        for t in range(2 * hf, min(nt, 2 * hf + 2)):
                            last = pe.transpose(Y[i][0:NE, (t % 2) * P:(t % 2 + 1) * P], wg[:, t, :], ident[:, :])
                        last.then_inc(y_full, 1)
                if s < NE:
                    layer(w1, hT, s, done1, None)
                if 0 < s <= NE:
                    layer(w2, h1[:, (s - 1) % 2, :, :], s - 1, done2, done1[s - 1])
                if s == NE and nxt:
                    turn(pe, z, nxt, g * 2 + 3)
                if s > 1:
                    e_ = s - 2
                    pe.wait_ge(z_free, done2[e_] + 4)
                    for hf in range((nt + 1) // 2):
                        i, no = y.take()
                        pe.wait_ge(y_free, no)
                        for t in range(2 * hf, min(nt, 2 * hf + 2)):
                            for k in range(2):
                                last = pe.matmul(Y[i][:, (t % 2) * D:(t % 2 + 1) * D], h2[:, e_ % 2, k, t * P:(t + 1) * P],
                                                 wo[:, e_, k, :], start=k == 0, stop=k == 1)
                        last.then_inc(y_full, 1)
                hook(f"s{s}")
            pe.wait_ge(wT_ready, g + 1)
            for hf in range((nt + 1) // 2):
                i, no = y.take()
                pe.wait_ge(y_free, no)
                for t in range(2 * hf, min(nt, 2 * hf + 2)):
                    last = pe.matmul(Y[i][:, (t % 2) * D:(t % 2 + 1) * D], wT[:, t * P:(t + 1) * P], bo, start=True, stop=True)
                last.then_inc(y_full, 1)
            assert not nxt or (z.n, y.n) == (ZF + 2, YF), (z.n, y.n)

        def grp_act(act, g, nt, hook, agg_wait, nxt, col0=0, shift=False):
            z = Fill(g, ZF, 4, 2)
            N = nt * P
            s_ = nc.scalar

            def drain(dst_, f, wide=N):
                i, no = z.take()
                act.wait_ge(z_full, no)
                f(dst_, Z[i][:, 0:wide]).then_inc(z_free, 1)

            def copy(o, i_):
                return s_.activation(o, i_, ACT.Copy)

            act.wait_ge(*agg_wait)
            copy(aT[:, :, 0:N], aggT[:, :, col0:col0 + N])
            copy(aC[:, 0:N], aggC[:, col0:col0 + N]).then_inc(at_ready, 1)
            if shift:
                act.wait_ge(at_ready, g + 1)
                copy(agg[:, :, 0:T], agg[:, :, T:2 * T]).then_inc(shifted, 1)
                act.wait_ge(shifted, g * 3 + 1)
                copy(agg[:, :, T:2 * T], agg[:, :, 2 * T:3 * T]).then_inc(shifted, 1)
                act.wait_ge(shifted, g * 3 + 2)
                copy(agg[:, :, 2 * T:3 * T], zeros[:, :, :]).then_inc(shifted, 1)
            act.wait_ge(dd_in, g + 1)
            s_.activation(dd[:, 0:nt], dd[:, 0:nt], ACT.Sqrt).then_inc(dd_sd, 1)
            hook("A")
            act.wait_ge(var_in, g + 1)
            s_.activation(rs[:, 0:nt], rs[:, 0:nt], ACT.Sqrt).then_inc(var_sd, 1)
            for k in range(2):
                drain(hT[:, k, 0:N], copy)
            hook("B1")
            act.wait_ge(sm_in, g + 1)
            s_.activation(wg[:, 0:nt, :], wg[:, 0:nt, :], ACT.Exp).then_inc(sm_exp, 1)

            def layer(l, e_, o):
                for m in range(2):
                    c = e_ * 2 + m
                    drain(o[:, m, 0:N], lambda d_, i_: s_.activation(
                        d_, i_, ACT.Relu, bias=bns[:, l, 1, c:c + 1], scale=bns[:, l, 0, c:c + 1]))

            for s in range(NE + 2):
                if s < NE:
                    layer(0, s, h1[:, s % 2, :, :])
                if 0 < s <= NE:
                    layer(1, s - 1, h2[:, (s - 1) % 2, :, :])
                if s == NE and nxt:
                    N = nxt * P
                    for k in range(2):
                        drain(hT[:, k, 0:N], copy, N)
                hook(f"s{s}")

        def norm_x(dve, g, nt, link):
            v = nc.vector
            v.tensor_copy(gm[:, 0, 0:nt], mean[:, ds(g * GT, nt)])
            link(v.tensor_copy(gm[:, 1, 0:nt], rstd[:, ds(g * GT, nt)]))
            dve.wait_ge(x_loaded, g * 16 + 16)
            for t in range(nt):
                last = v.tensor_scalar(hg[:, t, :], xg[:, t, :], gm[:, 0, t:t + 1], gm[:, 1, t:t + 1], ALU.add, ALU.mult)
            last.then_inc(hg_ready, 1)
            dve.wait_ge(hg_ready, g * 2 + 1)
            link(v.tensor_tensor(xg[:, 0:nt, :], xg[:, 0:nt, :], ub_all[:, :].unsqueeze(1).to_broadcast([P, nt, D]), ALU.add))

        def grp_dve(dve, g, nt, hook, own, g0, per, nxt, shift=False):
            y = Fill(g, YF, 2)
            v = nc.vector
            count = [0]
            base = (g - g0) * per

            def mark(ins):
                count[0] += 1
                ins.then_inc(own, 1)
                return count[0]

            def since(c):
                dve.wait_ge(own, base + c)

            def link(ins):
                since(mark(ins))

            def full():
                i, no = y.take()
                dve.wait_ge(y_full, no)
                return Y[i]

            b = full()
            v.tensor_scalar(dd[:, 0:nt], b[:, 0:nt], 1.0, None, ALU.max).then_inc(dd_in, 1)
            dve.wait_ge(dd_in, g + 1)
            dve.sem_inc(y_free, 1)
            if shift:
                dve.wait_ge(shifted, g * 3 + 3)
            hook("A")
            dve.wait_ge(dd_sd, g + 1)
            link(v.reciprocal(dd[:, 0:nt], dd[:, 0:nt]))
            dve.wait_ge(out_stored, g * 16 + 16)
            marks = {}
            for t in range(nt):
                b = full()
                link(v.scalar_tensor_tensor(out=acc[:, t, :], in0=b[:, D:2 * D], scalar=dd[:, t:t + 1], in1=xg[:, t, :],
                                            op0=ALU.mult, op1=ALU.add))
                v.tensor_tensor(acc[:, t, :], acc[:, t, :], b[:, 0:D], ALU.add).then_inc(y_free, 1)
            v.sem_inc(xg_free, 1)
            dve.wait_ge(y_free, y.base + y.n + 2)
            for t in range(nt):
                m_ = mark(v.bn_stats(st[:, t, :], acc[:, t, :]))
            since(m_)
            dve.sem_inc(measured, 1)
            for t in range(nt):
                m_ = mark(v.bn_aggr(mv[:, t, :], st[:, t, :]))
            since(m_)
            v.tensor_scalar(rs[:, 0:nt], mv[:, 0:nt, 1:2].rearrange("p t o -> p (t o)"), LN_EPS, None, ALU.add).then_inc(var_in, 1)
            dve.wait_ge(var_sd, g + 1)
            link(v.reciprocal(rs[:, 0:nt], rs[:, 0:nt]))
            for t in range(nt):
                last = v.tensor_scalar(hg[:, t, :], acc[:, t, :], mv[:, t, 0:1], rs[:, t:t + 1], ALU.subtract, ALU.mult)
            last.then_inc(hg_ready, 1)
            hook("B1")
            b = full()
            lg = b[:, 0:nt * NE].rearrange("p (t e) -> p t e", e=NE)
            link(v.tensor_tensor(wg[:, 0:nt, :], lg, br_all[:, :].unsqueeze(1).to_broadcast([P, nt, NE]), ALU.add))
            dve.sem_inc(y_free, 1)
            link(v.reduce_max(mx[:, 0:nt], wg[:, 0:nt, :], AX.X))
            link(v.tensor_tensor(wg[:, 0:nt, :], wg[:, 0:nt, :], mx[:, 0:nt].unsqueeze(2).to_broadcast([P, nt, NE]), ALU.subtract))
            dve.sem_inc(sm_in, 1)
            dve.wait_ge(sm_exp, g + 1)
            link(v.reduce_sum(mx[:, 0:nt], wg[:, 0:nt, :], AX.X))
            link(v.reciprocal(mx[:, 0:nt], mx[:, 0:nt]))
            v.tensor_tensor(wg[:, 0:nt, :], wg[:, 0:nt, :], mx[:, 0:nt].unsqueeze(2).to_broadcast([P, nt, NE]),
                            ALU.mult).then_inc(wg_ready, 1)
            dve.wait_ge(wg_ready, g + 1)
            if nxt:
                norm_x(dve, g + 1, nxt, link)
            m_acc = {}
            for s in range(NE + 2):
                if s == 2:
                    for hf in range((nt + 1) // 2):
                        b = full()
                        w_ = min(nt - 2 * hf, 2) * P
                        last = v.tensor_copy(wT[:, hf * 2 * P:hf * 2 * P + w_], b[0:NE, 0:w_])
                        last.then_inc(y_free, 1)
                    dve.wait_ge(y_free, y.base + y.n + 2)
                    dve.sem_inc(wT_ready, 1)
                if s > 1:
                    e_ = s - 2
                    for hf in range((nt + 1) // 2):
                        b = full()
                        if hf in m_acc:
                            since(m_acc[hf])
                        for t in range(2 * hf, min(nt, 2 * hf + 2)):
                            last = v.scalar_tensor_tensor(out=acc[:, t, :], in0=b[:, (t % 2) * D:(t % 2 + 1) * D],
                                                          scalar=wg[:, t, e_:e_ + 1], in1=acc[:, t, :],
                                                          op0=ALU.mult, op1=ALU.add)
                            if t < min(nt, 2 * hf + 2) - 1:
                                continue
                            m_acc[hf] = mark(last)
                        since(m_acc[hf])
                        dve.sem_inc(y_free, 1)
                hook(f"s{s}")
            for hf in range((nt + 1) // 2):
                b = full()
                w_ = min(nt - 2 * hf, 2) * D
                o = acc[:, 2 * hf:min(nt, 2 * hf + 2), :].rearrange("p t d -> p (t d)")
                v.tensor_tensor(o, o, b[:, 0:w_], ALU.add).then_inc(y_free, 1)
            dve.wait_ge(y_free, y.base + y.n + 2)
            dve.sem_inc(out_ready, 1)
            assert not nxt or count[0] == per, count[0]

        PER = 1 + GT + 2 * GT + 1 + 5 + 2 + GT // 2 * NE

        SCAN = NSB * NW

        def each_group(eng, scan, emit):
            with eng.Fori(0, NG - 2) as g:
                scan(g)
                emit(g, GT, 0, GT)
            for i in range(2):
                scan(NG - 2 + i)
                emit(NG - 2 + i, (GT, 1)[i], 1, (1, 0)[i])

        def branches(eng, fast, general):
            broken = eng.value_load(flag_i[0:1, 0:1], min_val=-NP, max_val=NP)
            with eng.If(broken > 0):
                general()
            with eng.Else():
                fast()

        with nc.Block() as block:
            @block.sync
            def _(sp):
                load_x(sp, 0, GT)
                sp.sem_inc(out_stored, 16)
                with sp.Fori(0, NG - 2) as g:
                    grp_sp(sp, g, GT, GT)
                grp_sp(sp, NG - 2, GT, 1)
                grp_sp(sp, NG - 1, 1, 0)
                sp.wait_ge(out_stored, 16 * NG + 16)

            @block.gpsimd
            def _(pool):
                def fast():
                    for J in range(GS + LEAD):
                        sb_pool(pool, J, J, lambda s, b: (src, typ)[s][:, J * SB + b:J * SB + b + 1])
                    with pool.Fori(1, NG - 1) as k:
                        for j in range(GS):
                            if j % HG == 0:
                                if j == 0:
                                    pool.wait_ge(idx_put, k * 2 - 1)
                                else:
                                    pool.wait_ge(idx_put, k * 2)
                            sb_pool(pool, k * GS + (LEAD + j), j, lambda s, b: idx[:, j // HG, s, (j % HG) * SB + b:(j % HG) * SB + b + 1])

                    sb_pool(pool, NSB, NSB, lambda s, b: (src, typ)[s][:, NSB * SB + b:NSB * SB + b + 1])

                def general():
                    def scan(g):
                        with pool.Fori(0, NSB) as J:
                            pool.wait_ge(g_idx, g * NSB + J + 1)
                            pool.sem_inc(issued, 1)
                            for b in range(SB):
                                for tab, dst_, s in ((rtab, R, 1), (htab, H, 0)):
                                    pool.indirect_dma_start(
                                        out=dst_[:, 0, b * DX:(b + 1) * DX], out_offset=None, in_=tab,
                                        in_offset=bass.IndirectOffsetOnAxis(ap=idx[:, 0, s, b:b + 1], axis=0)).then_inc(g_gath, 16)

                    each_group(pool, scan, lambda g, nt, i, nxt: None)

                branches(pool, fast, general)

            @block.scalar
            def _(act):
                def fast():
                    split_hi(act, 0, 0)
                    for J in range(GS + LEAD):
                        sb_act(act, J, J)
                    with act.Fori(1, NG - 1) as k:
                        hook = lambda p: p in POS and sb_act(act, k * GS + (LEAD + POS.index(p)), POS.index(p))
                        grp_act(act, k - 1, GT, hook, (added, k * GS + (LEAD - 1)), GT, 0, True)
                    grp_act(act, NG - 2, GT, none, (added, NSB), 1)
                    grp_act(act, NG - 1, 1, none, (added, NSB), 0, T)

                def general():
                    def scan(g):
                        with act.Fori(0, NSB) as J:
                            act.wait_ge(prod, g * NSB + J + 1)
                            nc.scalar.activation(Xh[:, 0, :], H[:, 0, :], ACT.Copy).then_inc(hi_done, 1)
                            with act.Fori(0, NW) as w:
                                act.wait_ge(g_mm, g * SCAN + J * NW + w + 1)
                                nc.scalar.activation(Psb[:, 0, 0:D + 2], PA[0:W, 0:D + 2], ACT.Copy).then_inc(g_ev, 1)

                    each_group(act, scan, lambda g, nt, i, nxt: grp_act(act, g, nt, none, (g_add, g * SCAN + SCAN), nxt))

                z = Fill(0, ZF, 4)
                for k in range(2):
                    i, no = z.take()
                    act.wait_ge(z_full, no)
                    nc.scalar.activation(hT[:, k, :], Z[i][:, 0:T], ACT.Copy).then_inc(z_free, 1)
                branches(act, fast, general)

            @block.tensor
            def _(pe):
                def fast():
                    for J in range(GS + LEAD):
                        sb_pe(pe, J, J)
                    with pe.Fori(1, NG - 1) as k:
                        hook = lambda p: p in POS and sb_pe(pe, k * GS + (LEAD + POS.index(p)), POS.index(p))
                        grp_pe(pe, k - 1, GT, hook, GT)
                    sb_turn(pe, NSB - 1, NSB - 1)
                    grp_pe(pe, NG - 2, GT, none, 1)
                    grp_pe(pe, NG - 1, 1, none, 0)

                def general():
                    def scan(g):
                        with pe.Fori(0, NSB) as J:
                            with pe.Fori(0, NW) as w:
                                at = g * SCAN + J * NW + w + 1
                                pe.wait_ge(g_s, at)
                                for b in range(SB):
                                    for x in (Xh, Xl):
                                        last = pe.matmul(PA[0:W, 0:D + 2], S[:, 0, b, :], x[:, 0, b * DX:b * DX + D + 2],
                                                         start=b == 0 and x is Xh, stop=b == SB - 1 and x is Xl)
                                last.then_inc(g_mm, 1)
                                pe.wait_ge(g_ev, at)
                                pe.sem_inc(turning, 1)
                                for k, (lo, hi) in enumerate(((0, P), (P, D), (D, D + 2))):
                                    last = pe.transpose(PT[0:hi - lo, k * W:(k + 1) * W], Psb[:, 0, lo:hi], ident[0:W, 0:W])
                                last.then_inc(g_tr, 1)

                    each_group(pe, scan, lambda g, nt, i, nxt: grp_pe(pe, g, nt, none, nxt))

                turn(pe, Fill(0, ZF, 4), GT, 1)
                branches(pe, fast, general)

            @block.vector
            def _(dve):
                v = nc.vector
                dve.sem_inc(z_free, 4)
                dve.sem_inc(y_free, 2)
                first = [0]

                def link(ins):
                    first[0] += 1
                    ins.then_inc(f_own[3], 1)
                    dve.wait_ge(f_own[3], first[0])

                link(v.memset(zeros[:, :, :], 0.0))
                norm_x(dve, 0, GT, link)

                def fast():
                    dve.sem_inc(idx_put, 2)
                    sb_product(dve, 0, 0)
                    split_lo(dve, 0, 0)
                    for J in range(GS + LEAD):
                        sb_dve(dve, J, J)
                    with dve.Fori(1, NG - 1) as k:
                        def hook(p):
                            if p not in POS:
                                return
                            j = POS.index(p)
                            J = k * GS + (LEAD + j)
                            sb_dve(dve, J, j)
                            if j % HG == HG - 1:
                                hf = j // HG
                                for s, t in enumerate((src, typ)):
                                    last = v.tensor_copy(idx[:, hf, s, :], t[:, ds((k * GS + (LEAD + GS + HG * hf)) * SB, HG * SB)])
                                last.then_inc(idx_put, 1)

                        grp_dve(dve, k - 1, GT, hook, f_own[0], 0, PER, GT, True)
                    sb_add(dve, NSB - 1, NSB - 1)
                    grp_dve(dve, NG - 2, GT, none, f_own[1], NG - 2, PER, 1)
                    grp_dve(dve, NG - 1, 1, none, f_own[1], NG - 2, PER, 0)

                def general():
                    dl = dloc[:, 0:NB].rearrange("p (s b) -> p s b", b=SB)
                    link(v.tensor_tensor(dl, dl, PA[:, 0:NSB].unsqueeze(2).to_broadcast([P, NSB, SB]), ALU.add))
                    def scan(g):
                        with dve.Fori(0, NSB) as J:
                            for s, t in enumerate((src, typ)):
                                last = v.tensor_copy(idx[:, 0, s, 0:SB], t[:, ds(J * SB, SB)])
                            last.then_inc(g_idx, 1)
                            dve.wait_ge(g_gath, (g * NSB + J) * 128 + 128)
                            v.tensor_tensor(H[:, 0, :], H[:, 0, :], R[:, 0, :], ALU.mult).then_inc(prod, 1)
                            dve.wait_ge(hi_done, g * NSB + J + 1)
                            v.tensor_tensor(Xl[:, 0, :], H[:, 0, :], Xh[:, 0, :].bitcast(fp32), ALU.subtract)
                            v.tensor_copy(dwin[:, :], dloc[:, ds(J * SB, SB)]).then_inc(g_own, 1)
                            with dve.Fori(0, NW) as w:
                                at = g * SCAN + J * NW + w + 1
                                dve.wait_ge(g_own, g * (NSB * (NW + 1) + 2) + J * (NW + 1) + w + 1)
                                v.tensor_tensor(S[:, 0, :, :], dwin[:, :].unsqueeze(2).to_broadcast([P, SB, W]),
                                                iota_w[:, :].unsqueeze(1).to_broadcast([P, SB, W]), ALU.is_equal).then_inc(g_s, 1)
                                dve.wait_ge(g_s, at)
                                v.tensor_scalar(dwin[:, :], dwin[:, :], float(-W), None, ALU.add).then_inc(g_own, 1)
                                dve.wait_ge(g_tr, at)
                                w_ = aggT[:, :, ds(w * W, W)]
                                v.tensor_tensor(w_, w_, PT[:, 0:2 * W].rearrange("p (k w) -> p k w", k=2), ALU.add)
                                c_ = aggC[:, ds(w * W, W)]
                                v.tensor_tensor(c_, c_, PT[0:2, 2 * W:3 * W], ALU.add).then_inc(g_add, 1)
                                dve.wait_ge(g_add, at)
                        v.tensor_scalar(dloc[:, 0:NB], dloc[:, 0:NB], float(-T), None, ALU.add).then_inc(g_own, 1)
                        dve.wait_ge(at_ready, g + 1)
                        v.memset(agg[:, :, :], 0.0).then_inc(g_own, 1)
                        dve.wait_ge(g_own, (g + 1) * (NSB * (NW + 1) + 2))

                    each_group(dve, scan, lambda g, nt, i, nxt: grp_dve(dve, g, nt, none, f_own[i], i * (NG - 2), PER, nxt))

                branches(dve, fast, general)


def layout(x, src, dst, edge_type_500, L0_gnn_relation_emb, L0_gnn_msg_w, L0_gnn_msg_b, L0_gnn_upd_w,
           L0_gnn_upd_b, L0_gnn_gate_w, L0_gnn_gate_b, **f):
    n, e, nrel = x.shape[0], src.shape[0], L0_gnn_relation_emb.shape[0]
    nt, ng, nsb = sizes(n, e)
    nb = nsb * SB

    def cols(v, fill, wide):
        v = np.asarray(v)
        o = np.full(wide * P, fill, v.dtype)
        o[:e] = v
        return np.ascontiguousarray(o.reshape(wide, P).T)

    dst = np.asarray(dst)
    wide = nb + GS * SB
    x = np.asarray(x)
    xp = np.zeros((nt * P, D), x.dtype)
    xp[:n] = x
    at = ((0, 1, 2, 3), (1, 0, 3, 2), (2, 3, 0, 1), (3, 2, 1, 0))
    mw, uw = np.asarray(L0_gnn_msg_w), np.asarray(L0_gnn_upd_w)
    km = np.concatenate([np.concatenate([mw[i] for i in row], 1) for row in at], 0)
    u = np.concatenate([np.concatenate([uw[i] for i in row], 1) for row in at], 0)
    ut = u.T.reshape(D, 4, 64).transpose(0, 2, 1).reshape(D, D)
    g = {k[len("L0_ffn_"):]: np.asarray(v) for k, v in f.items()}
    bn = np.stack([np.stack([g[k + str(l)].reshape(NE * 2, P).T for k in ("b", "g", "be", "m", "v")], 1) for l in (1, 2)], 1)
    return {
        "x": xp, "src": cols(src, n, wide), "typ": cols(edge_type_500, nrel, wide), "dst": cols(dst, dst[-1], nb),
        "rel": np.asarray(L0_gnn_relation_emb),
        "gw": np.asarray(L0_gnn_gate_w).reshape(64, 4).T.reshape(D), "gb": np.asarray(L0_gnn_gate_b),
        "km": km, "ut": ut, "mb": np.asarray(L0_gnn_msg_b).reshape(2, P).T,
        "ub": np.asarray(L0_gnn_upd_b).T.reshape(D),
        "bn": bn, "wr": g["Wr"], "br": g["br"], "bo": g["bo"],
        "w1": g["W1"], "w2": g["W2"], "wo": g["Wo"],
    }, n, e, nrel


def kernel(**inputs):
    import concourse.bacc as bacc
    from concourse.bass_utils import run_bass_kernel_spmd

    data, n, e, nrel = layout(**inputs)
    nc = bacc.Bacc("TRN2", target_bir_lowering=False, num_devices=1)
    arrays = {f"in_{k}": np.ascontiguousarray(v) for k, v in data.items()}
    aps = {k[3:]: nc.dram_tensor(k, v.shape, mybir.dt.from_np(v.dtype), kind="ExternalInput").ap() for k, v in arrays.items()}
    out = nc.dram_tensor("out", (n, D), mybir.dt.float32, kind="ExternalOutput").ap()
    build(nc, aps, out, n, e, nrel)
    r = run_bass_kernel_spmd(nc, [arrays], core_ids=[0])
    return r.results[0]["out"]
```

```python
from contextlib import ExitStack

import numpy as np
import concourse.bass as bass
from concourse import mybir

P = 128
D = 256
DX = 260
NE = 8
W = 64
SB = 4
GT = 2
GS = 8
PRE = 3
LEAD = 2
REST = 2
LN_EPS = 1e-5
BN_EPS = 1e-3
NEG = ((0, 3), (1, 2), (2, 3))


def sizes(n, e):
    nt = -(-n // P)
    ng = nt // GT
    nsb = GS * ng + LEAD + REST
    assert nt == GT * ng + 1 and 0 <= nsb * SB * P - e, (nt, ng, nsb, e)
    return nt, ng, nsb


def build(nc, a, out, n, e, nrel):
    fp32, f32r, i32, bf16 = mybir.dt.float32, mybir.dt.float32r, mybir.dt.int32, mybir.dt.bfloat16
    ALU, ACT, AX = mybir.AluOpType, mybir.ActivationFunctionType, mybir.AxisListType
    NT, NG, NSB = sizes(n, e)
    NB = NSB * SB
    NBI = NB + GS * SB
    NP = NT * P
    RT = nrel // 4
    T = GT * P
    LT = GT + 1
    TL = LT * P
    AW = 3 * T
    NW = T // W
    NWL = TL // W
    HB = max(h for h in range(1, 17) if NB % (2 * h) == 0)
    ds = bass.ds

    htab = nc.dram_tensor("h_table", [NP, DX], fp32, kind="Internal").ap()
    rtab = nc.dram_tensor("r_table", [nrel + 1, DX], fp32, kind="Internal").ap()

    ctx = ExitStack()
    with ctx:
        def sb(name, shape, dt=fp32):
            return ctx.enter_context(nc.sbuf_tensor(name, shape, dt))

        def sem(name):
            return ctx.enter_context(nc.semaphore(name))

        agg = sb("agg", [P, 3, AW])
        aggT = agg[:, 0:2, :]
        aggC = agg[0:2, 2, :]
        early = ExitStack()

        def sb0(name, shape, dt=fp32):
            return early.enter_context(nc.sbuf_tensor(name, shape, dt))

        w1, w2, wo = (sb(x, [P, NE, 2, D]) for x in ("w1", "w2", "wo"))
        H = sb("H", [P, 4, SB * DX])
        R = sb("R", [P, 4, SB * DX])
        src = sb("src", [P, NBI], i32)
        typ = sb("typ", [P, NBI], i32)
        idx = sb("idx", [P, 2, 2, GS * SB // 2], i32)
        dloc = sb("dloc", [P, NB + SB])
        dwin = sb("dwin", [P, SB])
        S = sb("S", [P, 2, SB, W], f32r)
        Psb = sb("Psb", [W, 2, DX])
        xg = sb("xg", [P, LT, D])
        acc = sb("acc", [P, LT, D])
        hg = sb("hg", [P, LT, D])
        hT = sb("hT", [P, 2, TL])
        aT = sb("aT", [P, 2, TL])
        aC = sb("aC", [2, TL])
        h1 = sb("h1", [P, 2, 2, TL])
        h2 = sb("h2", [P, 2, 2, TL])
        UT = sb("UT", [P, 2, D])
        W2T = sb("W2T", [P, 2, D])
        umb = sb("umb", [2, D])
        ub_all = sb("ub_all", [P, D])
        br_all = sb("br_all", [P, NE])
        wr = sb("wr", [P, 2, NE])
        few = sb("few", [P, D + TL])
        bo = few[32:32 + NE, 0:D]
        wT = few[32:32 + NE, D:D + TL]
        base_i = few[96:97, 0:NSB].bitcast(i32)
        bns = sb("bns", [P, 2, 2, NE * 2])
        ident = sb("ident", [P, P])
        iota_w = sb("iota_w", [P, W])
        sel = sb("sel", [2, 1])
        mean = sb("mean", [P, NT + GT])
        rstd = sb("rstd", [P, NT + GT])
        flag = sb("flag", [P, 4])
        flag_i = sb("flag_i", [1, 1], i32)
        gm = sb("gm", [P, 2, LT])
        dd = sb("dd", [P, LT])
        st = sb("st", [P, LT, 6])
        mv = sb("mv", [P, LT, 2])
        rs = sb("rs", [P, LT])
        mx = sb("mx", [P, LT])
        wg = sb("wg", [P, LT, NE])
        xall = sb0("xall", [P, NT, DX])
        small = sb0("small", [P, P + 2 * NT])
        rext = sb0("rext", [P, 4, DX])
        rflat = R[:, :, :].rearrange("p a b -> p (a b)")
        words = HB * P // 2
        hwords = (HB * NT + 1) // 2
        oh_lo = [rflat[:, i * words:(i + 1) * words].bitcast(bf16)
                 .rearrange("p (c b) -> p c b", b=HB) for i in range(2)]
        iota_cb = rflat[:, 2 * words:3 * words].bitcast(bf16).rearrange("p (c b) -> p c b", b=HB)
        oh_hi = [rflat[:, 3 * words + i * hwords:3 * words + (i + 1) * hwords].bitcast(bf16)[:, 0:HB * NT]
                 .rearrange("p (c b) -> p c b", b=HB) for i in range(2)]
        dst_at = 3 * words + 2 * hwords
        dst_i = rflat[:, dst_at:dst_at + NB].bitcast(i32)
        hflat = H[:, :, :].rearrange("p a b -> p (a b)")
        lo_b = hflat[:, 0:NB // 2].bitcast(bf16)
        hi_b = hflat[:, NB:NB + NB // 2].bitcast(bf16)
        lo_i = hflat[:, 2 * NB:3 * NB].bitcast(i32)
        hi_i = hflat[:, 3 * NB:4 * NB].bitcast(i32)
        col = acc[0:1, 2, 0:NSB]
        h1flat = h1[:, :, :, :].rearrange("p a b c -> p (a b c)")
        h2flat = h2[:, :, :, :].rearrange("p a b c -> p (a b c)")
        rel = h1flat[:, 0:4 * D].rearrange("p (k c) -> p k c", k=4)
        tmp = h1flat[:, 0:NB]
        viol = h2flat[:, 0:NB]
        bn = h2flat[:, NB:NB + 10 * NE * 2].rearrange("p (l q c) -> p l q c", l=2, q=5)
        ones0 = h2flat[0:1, NB + 20 * NE:NB + 20 * NE + P]
        gwb = hg[:, 0, :]
        rprod = hg[:, 1, :]
        zrow = hT[0:1, :, :].rearrange("p a b -> p (a b)")[:, 0:DX]
        km = aT
        mb = acc[:, 0, 0:2]
        gbc = acc[:, 0, 2:3]
        gate = acc[:, 0, 4:8]
        egate = acc[:, 0, 8:12]
        iota_f = small[:, 0:P]
        sq = xg[:, 0, :]
        ssum = small[:, P:P + NT]
        ssq = small[:, P + NT:]
        dsr = acc[:, 1, 0:NT]
        hsc = acc[:, 1, 64:64 + NT]
        hbi = acc[:, 1, 128:128 + NT]

        def bank(name):
            return ctx.enter_context(nc.psum_tensor(name, [P, 512], fp32))

        Z = [bank(f"z{i}") for i in range(4)]
        Y = [bank("y0"), bank("y1")]
        PA = bank("pa")
        PT = bank("pt")

        gath = [sem(f"gathered{i}") for i in range(4)]
        prod, hi_done, lo_done = sem("products"), sem("products_hi"), sem("products_lo")
        issued = sem("superblocks_issued")

        def wait(eng, s, J, v):
            if isinstance(v, int) and v <= 0:
                return
            eng.wait_ge(s, v)

        def fill_no(J, j, d=0):
            if isinstance(J, int):
                return 128 * ((J + d) // 4 + 1)
            return (J - j) * 32 + 128 * ((j + d) // 4 + 1)

        def sb_pool(pool, J, j, cols):
            wait(pool, lo_done, J, J - 3)
            pool.sem_inc(issued, 1)
            for b in range(SB):
                for tab, dst_, ix in ((rtab, R[:, j % 4, b * DX:(b + 1) * DX], cols(1, b)),
                                      (htab, H[:, j % 4, b * DX:(b + 1) * DX], cols(0, b))):
                    pool.indirect_dma_start(out=dst_, out_offset=None, in_=tab,
                                            in_offset=bass.IndirectOffsetOnAxis(ap=ix, axis=0)).then_inc(gath[j % 4], 16)

        ld_idx, ld_dst, ld_rel, ld_cl, ld_bn, ld_ffn = (sem(x) for x in
            ("ld_idx", "ld_dst", "ld_rel", "ld_clifford", "ld_bn", "ld_experts"))
        ld_x = sem("ld_x")
        gated, hsc_ready, hscaled_act = sem("gated"), sem("h_scales"), sem("h_scaled_act")
        ld_typ = sem("ld_typ")
        consts, iotas = sem("consts"), sem("iotas")
        bins, oh_lo_done, oh_hi_done, oh_used, deg_done = (sem(x) for x in
            ("bins", "oh_lo_done", "oh_hi_done", "oh_used", "deg_done"))
        stats, ln_var, ln_sd, hscaled, tab_h, tab_r, r_ready, z_ready = (sem(x) for x in
            ("stats", "ln_var", "ln_sd", "hscaled", "tab_h", "tab_r", "r_ready", "z_ready"))
        gsum, gexp, cl_ready, w2_mm, base_mm, base_row, bn_in, bn_sd, ds_in, ds_sd = (sem(x) for x in
            ("gate_sum", "gate_exp", "clifford_ready", "w2_mm", "base_mm", "base_row",
             "bn_in", "bn_sd", "ds_in", "ds_sd"))
        z_dve, flag_in, flag_all, flag_done, tabs = (sem(x) for x in
            ("startup_dve", "flag_in", "flag_all", "flag_done", "tables"))
        act_own, pool_own, z_row = sem("startup_act"), sem("startup_pool"), sem("zero_row")
        HIT = NB // (2 * HB)
        assert HIT * 2 * HB == NB
        XC = 7
        NC = NT // XC if NT % XC == 0 else 1
        XN = NT // NC
        XD = (4 * XN + 6) // 7

        with nc.Block() as block:
            @block.sync
            def _(sp):
                sp.dma_start(src[:, :], a["src"]).then_inc(ld_idx, 16)
                sp.dma_start(dst_i, a["dst"]).then_inc(ld_dst, 16)
                sp.dma_start(rel[0:RT, :, :], a["rel"].rearrange("(k p) d -> p k d", k=4)).then_inc(ld_rel, 16)
                sp.dma_start(gwb[0:RT, :], a["gw"].partition_broadcast(RT)).then_inc(ld_rel, 16)
                sp.dma_start(gbc[0:RT, :], a["gb"].partition_broadcast(RT)).then_inc(ld_rel, 16)
                xv = a["x"].rearrange("(t p) d -> p t d", p=P)
                for c in range(NC):
                    sp.dma_start(xall[:, c * XN:(c + 1) * XN, 0:D], xv[:, c * XN:(c + 1) * XN, :]).then_inc(ld_x, 16)
                sp.dma_start(typ[:, :], a["typ"]).then_inc(ld_typ, 16)
                sp.dma_start(km[:, :, 0:D], a["km"].rearrange("(k p) d -> p k d", p=P)).then_inc(ld_cl, 16)
                sp.dma_start(UT[:, :, :], a["ut"].rearrange("(k p) d -> p k d", p=P)).then_inc(ld_cl, 16)
                sp.dma_start(mb, a["mb"]).then_inc(ld_cl, 16)
                sp.dma_start(ub_all[:, :], a["ub"].partition_broadcast(P)).then_inc(ld_cl, 16)
                sp.dma_start(bn[:, :, :, :], a["bn"]).then_inc(ld_bn, 16)
                sp.dma_start(wr[:, :, :], a["wr"].rearrange("(k p) d -> p k d", p=P)).then_inc(ld_ffn, 16)
                sp.dma_start(br_all[:, :], a["br"].partition_broadcast(P)).then_inc(ld_ffn, 16)
                sp.dma_start(bo, a["bo"]).then_inc(ld_ffn, 16)
                for t, name in ((w1, "w1"), (w2, "w2"), (wo, "wo")):
                    for i in range(NE):
                        sp.dma_start(t[:, i, :, :], a[name][i, :, :].rearrange("(k p) d -> p k d", p=P)).then_inc(ld_ffn, 16)
                sp.wait_ge(r_ready, 1)
                sp.dma_start(rtab[0:nrel, :].rearrange("(k p) c -> p k c", k=4), rext[0:RT, :, :]).then_inc(tab_r, 16)
                sp.wait_ge(z_row, 1)
                sp.dma_start(rtab[nrel:nrel + 1, :], zrow).then_inc(tab_r, 16)
                hv = htab.rearrange("(t p) c -> p t c", p=P)
                for c in range(NC):
                    sp.wait_ge(hscaled, c + 1)
                    sp.wait_ge(hscaled_act, c + 1)
                    sp.dma_start(hv[:, c * XN:(c + 1) * XN, :], xall[:, c * XN:(c + 1) * XN, :]).then_inc(tab_h, 16)
                sp.wait_ge(ld_ffn, 16 * (3 + 3 * NE))

            @block.gpsimd
            def _(pool):
                pool.iota(iota_f, pattern=[[1, P]], base=0, channel_multiplier=0,
                          allow_small_or_imprecise_dtypes=True).then_inc(iotas, 1)
                pool.iota(iota_cb, pattern=[[1, P], [0, HB]], base=0, channel_multiplier=0,
                          allow_small_or_imprecise_dtypes=True).then_inc(iotas, 1)
                pool.memset(ident[:, :], 0.0).then_inc(pool_own, 1)
                pool.wait_ge(pool_own, 1)
                pool.affine_select(out=ident[:, :], in_=ident[:, :], compare_op=ALU.not_equal, fill=1.0,
                                   base=0, pattern=[[-1, P]], channel_multiplier=1).then_inc(consts, 1)
                pool.memset(xall[:, :, D:DX], 0.0).then_inc(pool_own, 1)
                pool.wait_ge(pool_own, 2)
                pool.memset(xall[:, :, D + 1:D + 2], 1.0).then_inc(consts, 1)
                pool.memset(zrow, 0.0).then_inc(z_row, 1)
                pool.memset(rext[0:RT, :, D:DX], 0.0).then_inc(pool_own, 1)
                pool.wait_ge(gated, 1)
                pool.wait_ge(pool_own, 3)
                pool.memset(rext[0:RT, :, D + 1:D + 2], 1.0)
                pool.tensor_copy(rext[0:RT, :, D:D + 1].rearrange("p k o -> p (k o)"), gate[0:RT, :])
                for k in range(4):
                    last = pool.tensor_scalar(rext[0:RT, k, 0:D], rel[0:RT, k, :], gate[0:RT, k:k + 1], None, ALU.mult)
                last.then_inc(r_ready, 1)
                pool.wait_ge(ld_dst, 16)
                pool.memset(dloc[:, NB:NB + SB], 0.0)
                pool.tensor_copy(dloc[:, 0:NB], dst_i).then_inc(base_row, 1)
                pool.wait_ge(stats, 2)
                pool.tensor_scalar(rstd[:, 0:NT], ssq, 1.0 / D, LN_EPS, ALU.mult, ALU.add).then_inc(ln_var, 1)
                pool.wait_ge(tab_r, 32)
                pool.wait_ge(tab_h, 16 * NC)
                pool.wait_ge(ld_idx, 16)
                pool.wait_ge(ld_typ, 16)
                for J in range(PRE):
                    sb_pool(pool, J, J, lambda s, b: (src, typ)[s][:, J * SB + b:J * SB + b + 1])
                pool.wait_ge(flag_in, 1)
                pool.partition_all_reduce(flag[:, 1:2], flag[:, 0:1], P, bass.bass_isa.ReduceOp.max).then_inc(flag_all, 1)

            @block.scalar
            def _(act):
                own = [0]

                def link(ins):
                    own[0] += 1
                    ins.then_inc(act_own, 1)
                    act.wait_ge(act_own, own[0])

                act.wait_ge(gsum, 1)
                nc.scalar.activation(egate[0:RT, :], gate[0:RT, :], ACT.Exp, scale=-1.0).then_inc(gexp, 1)
                for c in range(NC):
                    act.wait_ge(ld_x, 16 * NC)
                    for t in range(c * XN, (c + 1) * XN):
                        last = nc.scalar.activation(sq, xall[:, t, 0:D], ACT.Copy, accum_out=ssum[:, t:t + 1])
                        link(last)
                act.mul(mean[:, 0:NT], ssum, -1.0 / D).then_inc(stats, 1)
                act.wait_ge(stats, 1)
                for t in range(NT):
                    link(nc.scalar.activation(sq, xall[:, t, 0:D], ACT.Square, bias=mean[:, t:t + 1],
                                              accum_out=ssq[:, t:t + 1]))
                act.sem_inc(stats, 1)
                act.wait_ge(ln_var, 1)
                nc.scalar.activation(rstd[:, 0:NT], rstd[:, 0:NT], ACT.Sqrt).then_inc(ln_sd, 1)
                act.wait_ge(ds_in, 1)
                nc.scalar.activation(dsr, dsr, ACT.Sqrt).then_inc(ds_sd, 1)
                act.wait_ge(hsc_ready, 1)
                for t in range(NT):
                    if t % XN >= XD:
                        last = nc.scalar.activation(xall[:, t, 0:D], xall[:, t, 0:D], ACT.Identity,
                                                    bias=hbi[:, t:t + 1], scale=hsc[:, t:t + 1])
                        if t % XN == XN - 1:
                            last.then_inc(hscaled_act, 1)
                act.wait_ge(bn_in, 1)
                nc.scalar.activation(bns[:, :, 0, :], bns[:, :, 0, :], ACT.Sqrt).then_inc(bn_sd, 1)

            @block.tensor
            def _(pe):
                pe.wait_ge(oh_lo_done, 1)
                with pe.Fori(0, HIT) as i:
                    for h in range(2):
                        pe.wait_ge(oh_lo_done, i * 2 + h + 2)
                        for b in range(HB):
                            last = pe.matmul(Y[0][:, 0:NT], oh_lo[h][:, :, b], oh_hi[h][:, :, b],
                                             start=False, stop=True, skip_group_check=True)
                        last.then_inc(oh_used, 1)
                pe.wait_ge(base_row, 1)
                pe.matmul(PA[:, 0:NSB], ones0, dloc[0:1, 0:NB:SB],
                          start=True, stop=True).then_inc(base_mm, 1)
                pe.wait_ge(cl_ready, 1)
                for m in range(2):
                    for k in range(2):
                        pe.matmul(Z[1][:, m * D:(m + 1) * D], km[:, k, m * P:(m + 1) * P], UT[:, k, :],
                                  start=k == 0, stop=k == 1)
                for k in range(2):
                    last = pe.matmul(Y[1][0:1, 0:D], mb[:, k:k + 1], UT[:, k, :], start=k == 0, stop=k == 1)
                last.then_inc(w2_mm, 1)

            @block.vector
            def _(dve):
                own = [0]

                def link(ins):
                    own[0] += 1
                    ins.then_inc(z_dve, 1)
                    dve.wait_ge(z_dve, own[0])

                v = nc.vector
                dve.wait_ge(ld_rel, 48)
                for k in range(4):
                    link(v.tensor_tensor(rprod[0:RT, :], rel[0:RT, k, :], gwb[0:RT, :], ALU.mult))
                    link(v.reduce_sum(gate[0:RT, k:k + 1], rprod[0:RT, :], AX.X))
                v.tensor_scalar(gate[0:RT, :], gate[0:RT, :], gbc[0:RT, :], None, ALU.add).then_inc(gsum, 1)
                dve.wait_ge(ld_idx, 16)
                dve.wait_ge(iotas, 2)
                v.memset(ones0, 1.0)
                v.tensor_copy(iota_w[:, :], iota_f[:, 0:W])
                v.tensor_scalar(lo_i, src[:, 0:NB], P - 1, None, ALU.bitwise_and)
                link(v.tensor_scalar(hi_i, src[:, 0:NB], 7, None, ALU.logical_shift_right))
                v.tensor_copy(lo_b, lo_i)
                v.tensor_copy(hi_b, hi_i).then_inc(bins, 1)
                v.memset(Y[0][:, 0:NT], 0.0).then_inc(oh_lo_done, 1)
                dve.sem_inc(oh_used, 2)
                dve.wait_ge(gexp, 1)
                link(v.tensor_scalar(egate[0:RT, :], egate[0:RT, :], 1.0, None, ALU.add))
                v.reciprocal(gate[0:RT, :], egate[0:RT, :]).then_inc(gated, 1)
                dve.wait_ge(bins, 1)
                with dve.Fori(0, HIT) as i:
                    for h in range(2):
                        dve.wait_ge(oh_used, i * 2 + h + 1)
                        for oh, part, m in ((oh_hi[h], hi_b, NT), (oh_lo[h], lo_b, P)):
                            last = v.tensor_tensor(oh, iota_cb[:, 0:m, :],
                                                   part[:, ds(i * (2 * HB) + h * HB, HB)].unsqueeze(1).to_broadcast([P, m, HB]),
                                                   ALU.is_equal)
                        last.then_inc(oh_lo_done, 1)
                dve.wait_ge(oh_used, 2 + 2 * HIT)
                v.tensor_scalar(dsr, Y[0][:, 0:NT], 1.0, None, ALU.max).then_inc(ds_in, 1)
                dve.wait_ge(ld_bn, 16)
                v.tensor_scalar(bns[:, :, 0, :], bn[:, :, 4, :], BN_EPS, None, ALU.add).then_inc(bn_in, 1)
                dve.wait_ge(ln_sd, 1)
                link(v.reciprocal(rstd[:, 0:NT], rstd[:, 0:NT]))
                dve.wait_ge(ds_sd, 1)
                link(v.reciprocal(dsr, dsr))
                link(v.tensor_tensor(hsc, rstd[:, 0:NT], dsr, ALU.mult))
                v.tensor_tensor(hbi, mean[:, 0:NT], hsc, ALU.mult).then_inc(hsc_ready, 1)
                dve.wait_ge(consts, 2)
                link(v.tensor_copy(xall[:, :, D:D + 1].rearrange("p t o -> p (t o)"), dsr))
                for t in range(NT):
                    if t % XN < XD:
                        last = v.tensor_scalar(xall[:, t, 0:D], xall[:, t, 0:D], hsc[:, t:t + 1], hbi[:, t:t + 1],
                                               ALU.mult, ALU.add)
                        if t % XN == XD - 1:
                            last.then_inc(hscaled, 1)
                dve.wait_ge(bn_sd, 1)
                link(v.reciprocal(bns[:, :, 0, :], bns[:, :, 0, :]))
                link(v.tensor_tensor(bns[:, :, 0, :], bns[:, :, 0, :], bn[:, :, 1, :], ALU.mult))
                link(v.tensor_tensor(bns[:, :, 1, :], bn[:, :, 0, :], bn[:, :, 3, :], ALU.subtract))
                link(v.tensor_tensor(bns[:, :, 1, :], bns[:, :, 1, :], bns[:, :, 0, :], ALU.mult))
                link(v.tensor_tensor(bns[:, :, 1, :], bns[:, :, 1, :], bn[:, :, 2, :], ALU.add))
                dve.wait_ge(ld_cl, 64)
                for b, q in NEG:
                    kb = km[(b % 2) * 64:(b % 2) * 64 + 64, b // 2, q * 64:q * 64 + 64]
                    v.tensor_scalar(kb, kb, -1.0, None, ALU.mult)
                    us = UT[(q % 2) * 64:(q % 2) * 64 + 64, q // 2, b:D:4]
                    last = v.tensor_scalar(us, us, -1.0, None, ALU.mult)
                last.then_inc(cl_ready, 1)
                dve.wait_ge(r_ready, 1)
                dve.wait_ge(base_row, 1)
                link(v.memset(tmp, 0.0))
                for g in range(NG - 1):
                    lo = (GS * (g + 1) + LEAD - 1) * SB
                    hi = (GS * (g + 2) + LEAD - 1) * SB if g < NG - 2 else NB
                    link(v.memset(tmp[:, lo:hi], float(T * (g + 1))))
                link(v.tensor_tensor(viol, tmp, dloc[:, 0:NB], ALU.subtract))
                link(v.tensor_scalar(col, viol[0:1, 0:NB:SB], -1.0, 0.0, ALU.mult, ALU.max))
                v.tensor_scalar(base_i, col, float(AW - W), None, ALU.min)
                link(v.tensor_scalar(tmp, viol, -1.0, float(W - AW), ALU.mult, ALU.add))
                link(v.tensor_tensor(viol, viol, tmp, ALU.max))
                dve.wait_ge(base_mm, 1)
                link(v.tensor_tensor(dloc[:, 0:NB].rearrange("p (s b) -> p s b", b=SB),
                                     dloc[:, 0:NB].rearrange("p (s b) -> p s b", b=SB),
                                     PA[:, 0:NSB].unsqueeze(2).to_broadcast([P, NSB, SB]), ALU.subtract))
                link(v.tensor_scalar(tmp, dloc[:, 0:NB], -1.0, None, ALU.mult))
                link(v.tensor_tensor(viol, viol, tmp, ALU.max))
                link(v.tensor_scalar(tmp, dloc[:, 0:NB], float(1 - W), None, ALU.add))
                link(v.tensor_tensor(viol, viol, tmp, ALU.max))
                v.reduce_max(flag[:, 0:1], viol, AX.X).then_inc(flag_in, 1)
                dve.wait_ge(flag_all, 1)
                v.tensor_copy(flag_i[:, :], flag[0:1, 1:2])
                dve.wait_ge(w2_mm, 1)
                v.tensor_copy(W2T[:, :, :], Z[1][:, :].rearrange("p (k d) -> p k d", k=2))
                link(v.memset(umb[:, :], 0.0))
                v.tensor_copy(umb[0:1, :], Y[1][0:1, 0:D])
                v.tensor_copy(sel[:, :], ident[0:2, 1:2])
                v.memset(agg[:, :, :], 0.0)
                v.tensor_copy(idx[:, 0, 0, :], src[:, (GS + LEAD + 0 * GS // 2) * SB:(GS + LEAD + 1 * GS // 2) * SB])
                v.tensor_copy(idx[:, 1, 0, :], src[:, (GS + LEAD + 1 * GS // 2) * SB:(GS + LEAD + 2 * GS // 2) * SB])
                dve.wait_ge(ld_typ, 16)
                v.tensor_copy(idx[:, 0, 1, :], typ[:, (GS + LEAD + 0 * GS // 2) * SB:(GS + LEAD + 1 * GS // 2) * SB])
                link(v.tensor_copy(idx[:, 1, 1, :], typ[:, (GS + LEAD + 1 * GS // 2) * SB:(GS + LEAD + 2 * GS // 2) * SB]))

        early.close()
        Xh = sb("Xh", [P, 2, SB * DX], f32r)
        Xl = sb("Xl", [P, 2, SB * DX], f32r)
        zeros = sb("zeros", [P, 3, T])
        shifted = sem("sums_shifted")
        s_ready, mm_done, p_evac, tr_done, added, idx_ok, idx_put = (sem(x) for x in
            ("onehots", "window_sums", "sums_copied", "sums_turned", "sums_added", "idx_used", "idx_put"))
        x_loaded, xg_free, z_full, z_free, y_full, y_free, hg_ready, at_ready = (sem(x) for x in
            ("x_loaded", "xg_free", "z_full", "z_free", "y_full", "y_free", "hg_ready", "at_ready"))
        dd_in, dd_sd, var_in, var_sd, sm_in, sm_exp, wg_ready, wT_ready, out_ready, out_stored = (sem(x) for x in
            ("dd_in", "dd_sd", "var_in", "var_sd", "sm_in", "sm_exp", "wg_ready", "wT_ready", "out_ready", "out_stored"))
        x_odd, ac_ready = sem("x_odd_loaded"), sem("counts_copied")
        turning, measured = sem("superblocks_turning"), sem("tiles_measured")
        f_own = [sem(f"vector_own{i}") for i in range(4)]
        g_idx, g_gath, g_s, g_mm, g_ev, g_tr, g_add, g_own = (sem(x) for x in
            ("g_idx", "g_gath", "g_s", "g_mm", "g_ev", "g_tr", "g_add", "g_own"))
        ZF = 4 + 4 * NE
        YF = 1 + GT + 1 + GT // 2 * (NE + 2)

        POS = ["A", "B1", "s0", "s2", "s3", "s5", "s6", "s8"]
        assert len(POS) == GS
        HG = GS // 2

        def sb_product(dve, J, j):
            dve.wait_ge(gath[j % 4], fill_no(J, j))
            nc.vector.tensor_tensor(H[:, j % 4, :], H[:, j % 4, :], R[:, j % 4, :], ALU.mult).then_inc(prod, 1)
            wait(dve, mm_done, J, J - 1)
            nc.vector.tensor_tensor(
                S[:, j % 2, :, :], dloc[:, ds(J * SB, SB)].unsqueeze(2).to_broadcast([P, SB, W]),
                iota_w[:, :].unsqueeze(1).to_broadcast([P, SB, W]), ALU.is_equal).then_inc(s_ready, 1)

        def split_hi(act, J, j):
            act.wait_ge(prod, J + 1)
            wait(act, mm_done, J, J - 1)
            nc.scalar.activation(Xh[:, j % 2, :], H[:, j % 4, :], ACT.Copy).then_inc(hi_done, 1)

        def split_lo(dve, J, j):
            dve.wait_ge(hi_done, J + 1)
            nc.vector.tensor_tensor(Xl[:, j % 2, :], H[:, j % 4, :], Xh[:, j % 2, :].bitcast(fp32), ALU.subtract).then_inc(lo_done, 1)

        def sb_add(dve, J, j):
            if isinstance(J, int) and J < 0:
                return
            at = dve.value_load(base_i[0:1, ds(J, 1)], min_val=0, max_val=AW - W)
            wait(dve, added, J, J)
            dve.wait_ge(tr_done, J + 1)
            w_ = aggT[:, :, ds(at, W)]
            nc.vector.tensor_tensor(w_, w_, PT[:, 0:2 * W].rearrange("p (k w) -> p k w", k=2), ALU.add)
            c_ = aggC[:, ds(at, W)]
            nc.vector.tensor_tensor(c_, c_, PT[0:2, 2 * W:3 * W], ALU.add).then_inc(added, 1)

        def sb_dve(dve, J, j, ahead=True):
            if ahead:
                sb_product(dve, J + 1, j + 1)
            sb_add(dve, J - 1, j - 1)
            if ahead:
                split_lo(dve, J + 1, j + 1)

        def sb_turn(pe, J, j):
            if isinstance(J, int) and J < 0:
                return
            pe.wait_ge(p_evac, J + 1)
            wait(pe, added, J, J)
            pe.sem_inc(turning, 1)
            for k, (lo, hi) in enumerate(((0, P), (P, D), (D, D + 2))):
                last = pe.transpose(PT[0:hi - lo, k * W:(k + 1) * W], Psb[:, j % 2, lo:hi], ident[0:W, 0:W])
            last.then_inc(tr_done, 1)

        def sb_pe(pe, J, j):
            sb_turn(pe, J - 1, j - 1)
            pe.wait_ge(s_ready, J + 1)
            wait(pe, p_evac, J, J)
            pe.wait_ge(lo_done, J + 1)
            for b in range(SB):
                for x in (Xh, Xl):
                    last = pe.matmul(PA[0:W, 0:D + 2], S[:, j % 2, b, :], x[:, j % 2, b * DX:b * DX + D + 2],
                                     start=b == 0 and x is Xh, stop=b == SB - 1 and x is Xl)
            last.then_inc(mm_done, 1)

        def sb_act(act, J, j, ahead=True):
            if ahead:
                split_hi(act, J + 1, j + 1)
            act.wait_ge(mm_done, J + 1)
            wait(act, tr_done, J, J - 1)
            nc.scalar.activation(Psb[:, j % 2, 0:D + 2], PA[0:W, 0:D + 2], ACT.Copy).then_inc(p_evac, 1)

        def none(pos):
            pass

        def grp_sp(sp, g, nt, nxt):
            if nxt:
                sp.wait_ge(xg_free, g + 1)
                load_x(sp, g + 1, nxt)
            sp.wait_ge(out_ready, g + 1)
            sp.dma_start(out[ds(g * T, T), :].rearrange("(t p) d -> p t d", p=P), acc[:, 0:GT, :]).then_inc(out_stored, 16)
            if nt > GT:
                rows = n - NG * T
                sp.dma_start(out[NG * T:n, :], acc[0:rows, GT, :]).then_inc(out_stored, 16)

        def load_x(sp, g, nt):
            sp.dma_start(xg[:, 0:nt, :], a["x"][ds(g * T, nt * P), :].rearrange("(t p) d -> p t d", p=P)).then_inc(x_loaded, 16)

        class Fill:
            def __init__(self, g, per, banks, first=0):
                assert per % banks == 0
                self.base, self.n, self.banks = g * per, first, banks

            def take(self):
                self.n += 1
                return (self.n - 1) % self.banks, self.base + self.n

        def turn(pe, z, nt, ready):
            pe.wait_ge(hg_ready, ready)
            for k in range(2):
                i, no = z.take()
                pe.wait_ge(z_free, no)
                for t in range(nt):
                    last = pe.transpose(Z[i][:, t * P:(t + 1) * P], hg[:, t, k * P:(k + 1) * P], ident[:, :])
                last.then_inc(z_full, 1)
            return no

        def grp_pe(pe, g, nt, hook, nxt):
            z, y = Fill(g, ZF, 4, 2), Fill(g, YF, 2)
            N = nt * P

            hook("A")
            pe.wait_ge(ac_ready, g + 1)
            i, no = y.take()
            pe.wait_ge(y_free, no)
            for t in range(nt):
                last = pe.matmul(Y[i][:, t:t + 1], aC[:, t * P:(t + 1) * P], sel[:, :], start=True, stop=True)
            last.then_inc(y_full, 1)
            pe.wait_ge(at_ready, g + 1)
            pe.wait_ge(z_free, z.base + 2 + 4)
            for t in range(nt):
                i, no = y.take()
                pe.wait_ge(y_free, no)
                c = slice(t * P, (t + 1) * P)
                pe.matmul(Y[i][:, 0:D], hT[:, 0, c], UT[:, 0, :], start=True, stop=False)
                pe.matmul(Y[i][:, 0:D], hT[:, 1, c], UT[:, 1, :], start=False, stop=True)
                pe.matmul(Y[i][:, D:2 * D], aT[:, 0, c], W2T[:, 0, :], start=True, stop=False)
                pe.matmul(Y[i][:, D:2 * D], aT[:, 1, c], W2T[:, 1, :], start=False, stop=False)
                pe.matmul(Y[i][:, D:2 * D], aC[:, c], umb[:, :], start=False, stop=True).then_inc(y_full, 1)
            hook("B1")
            zno = turn(pe, z, nt, g * 2 + 2)
            pe.wait_ge(z_free, zno + 4)
            i, no = y.take()
            pe.wait_ge(y_free, no)
            for t in range(nt):
                c = slice(t * P, (t + 1) * P)
                o = Y[i][:, t * NE:(t + 1) * NE]
                pe.matmul(o, hT[:, 0, c], wr[:, 0, :], start=True, stop=False)
                last = pe.matmul(o, hT[:, 1, c], wr[:, 1, :], start=False, stop=True)
            last.then_inc(y_full, 1)
            done1, done2 = {}, {}

            def layer(wt, x, e_, done, need):
                for m in range(2):
                    i, no = z.take()
                    pe.wait_ge(z_free, no)
                    if need is not None and m == 0:
                        pe.wait_ge(z_free, need + 4)
                    for k in range(2):
                        last = pe.matmul(Z[i][:, 0:N], wt[:, e_, k, m * P:(m + 1) * P], x[:, k, 0:N], start=k == 0, stop=k == 1)
                    last.then_inc(z_full, 1)
                    done[e_] = no

            for s in range(NE + 2):
                if s == 2:
                    pe.wait_ge(wg_ready, g + 1)
                    for hf in range((nt + 1) // 2):
                        i, no = y.take()
                        pe.wait_ge(y_free, no)
                        for t in range(2 * hf, min(nt, 2 * hf + 2)):
                            last = pe.transpose(Y[i][0:NE, (t % 2) * P:(t % 2 + 1) * P], wg[:, t, :], ident[:, :])
                        last.then_inc(y_full, 1)
                if s < NE:
                    layer(w1, hT, s, done1, None)
                if 0 < s <= NE:
                    layer(w2, h1[:, (s - 1) % 2, :, :], s - 1, done2, done1[s - 1])
                if s == NE and nxt:
                    turn(pe, z, nxt, g * 2 + 3)
                if s > 1:
                    e_ = s - 2
                    pe.wait_ge(z_free, done2[e_] + 4)
                    for hf in range((nt + 1) // 2):
                        i, no = y.take()
                        pe.wait_ge(y_free, no)
                        for t in range(2 * hf, min(nt, 2 * hf + 2)):
                            for k in range(2):
                                last = pe.matmul(Y[i][:, (t % 2) * D:(t % 2 + 1) * D], h2[:, e_ % 2, k, t * P:(t + 1) * P],
                                                 wo[:, e_, k, :], start=k == 0, stop=k == 1)
                        last.then_inc(y_full, 1)
                hook(f"s{s}")
            pe.wait_ge(wT_ready, g + 1)
            for hf in range((nt + 1) // 2):
                i, no = y.take()
                pe.wait_ge(y_free, no)
                for t in range(2 * hf, min(nt, 2 * hf + 2)):
                    last = pe.matmul(Y[i][:, (t % 2) * D:(t % 2 + 1) * D], wT[:, t * P:(t + 1) * P], bo, start=True, stop=True)
                last.then_inc(y_full, 1)
            assert not nxt or (z.n, y.n) == (ZF + 2, YF), (z.n, y.n)

        def grp_act(act, g, nt, hook, agg_wait, nxt, shift=False):
            z = Fill(g, ZF, 4, 2)
            N = nt * P
            s_ = nc.scalar

            def drain(dst_, f, wide=N):
                i, no = z.take()
                act.wait_ge(z_full, no)
                f(dst_, Z[i][:, 0:wide]).then_inc(z_free, 1)

            def copy(o, i_):
                return s_.activation(o, i_, ACT.Copy)

            act.wait_ge(*agg_wait)
            copy(aC[:, 0:N], aggC[:, 0:N]).then_inc(ac_ready, 1)
            copy(aT[:, :, 0:N], aggT[:, :, 0:N]).then_inc(at_ready, 1)
            if shift:
                act.wait_ge(at_ready, g + 1)
                copy(agg[:, :, 0:T], agg[:, :, T:2 * T]).then_inc(shifted, 1)
                act.wait_ge(shifted, g * 3 + 1)
                copy(agg[:, :, T:2 * T], agg[:, :, 2 * T:3 * T]).then_inc(shifted, 1)
                act.wait_ge(shifted, g * 3 + 2)
                copy(agg[:, :, 2 * T:3 * T], zeros[:, :, :]).then_inc(shifted, 1)
            act.wait_ge(dd_in, g + 1)
            s_.activation(dd[:, 0:nt], dd[:, 0:nt], ACT.Sqrt).then_inc(dd_sd, 1)
            hook("A")
            act.wait_ge(var_in, g + 1)
            s_.activation(rs[:, 0:nt], rs[:, 0:nt], ACT.Sqrt).then_inc(var_sd, 1)
            for k in range(2):
                drain(hT[:, k, 0:N], copy)
            hook("B1")
            act.wait_ge(sm_in, g + 1)
            s_.activation(wg[:, 0:nt, :], wg[:, 0:nt, :], ACT.Exp).then_inc(sm_exp, 1)

            def layer(l, e_, o):
                for m in range(2):
                    c = e_ * 2 + m
                    drain(o[:, m, 0:N], lambda d_, i_: s_.activation(
                        d_, i_, ACT.Relu, bias=bns[:, l, 1, c:c + 1], scale=bns[:, l, 0, c:c + 1]))

            for s in range(NE + 2):
                if s < NE:
                    layer(0, s, h1[:, s % 2, :, :])
                if 0 < s <= NE:
                    layer(1, s - 1, h2[:, (s - 1) % 2, :, :])
                if s == NE and nxt:
                    N = nxt * P
                    for k in range(2):
                        drain(hT[:, k, 0:N], copy, N)
                hook(f"s{s}")

        def norm_odd(dve, link):
            v = nc.vector
            dve.wait_ge(x_odd, 16)
            v.tensor_scalar(hg[:, GT, :], xg[:, GT, :], mean[:, NT - 1:NT], rstd[:, NT - 1:NT], ALU.add, ALU.mult)
            link(v.tensor_tensor(xg[:, GT, :], xg[:, GT, :], ub_all[:, :], ALU.add))

        def norm_x(dve, g, nt, link):
            v = nc.vector
            v.tensor_copy(gm[:, 0, 0:nt], mean[:, ds(g * GT, nt)])
            link(v.tensor_copy(gm[:, 1, 0:nt], rstd[:, ds(g * GT, nt)]))
            dve.wait_ge(x_loaded, g * 16 + 16)
            for t in range(nt):
                last = v.tensor_scalar(hg[:, t, :], xg[:, t, :], gm[:, 0, t:t + 1], gm[:, 1, t:t + 1], ALU.add, ALU.mult)
            last.then_inc(hg_ready, 1)
            dve.wait_ge(hg_ready, g * 2 + 1)
            link(v.tensor_tensor(xg[:, 0:nt, :], xg[:, 0:nt, :], ub_all[:, :].unsqueeze(1).to_broadcast([P, nt, D]), ALU.add))

        def grp_dve(dve, g, nt, hook, own, g0, per, nxt, shift=False):
            y = Fill(g, YF, 2)
            v = nc.vector
            count = [0]
            base = (g - g0) * per

            def mark(ins):
                count[0] += 1
                ins.then_inc(own, 1)
                return count[0]

            def since(c):
                dve.wait_ge(own, base + c)

            def link(ins):
                since(mark(ins))

            def full():
                i, no = y.take()
                dve.wait_ge(y_full, no)
                return Y[i]

            b = full()
            v.tensor_scalar(dd[:, 0:nt], b[:, 0:nt], 1.0, None, ALU.max).then_inc(dd_in, 1)
            dve.wait_ge(dd_in, g + 1)
            dve.sem_inc(y_free, 1)
            if shift:
                dve.wait_ge(shifted, g * 3 + 3)
            hook("A")
            dve.wait_ge(dd_sd, g + 1)
            link(v.reciprocal(dd[:, 0:nt], dd[:, 0:nt]))
            dve.wait_ge(out_stored, g * 16 + 16)
            marks = {}
            for t in range(nt):
                b = full()
                link(v.scalar_tensor_tensor(out=acc[:, t, :], in0=b[:, D:2 * D], scalar=dd[:, t:t + 1], in1=xg[:, t, :],
                                            op0=ALU.mult, op1=ALU.add))
                v.tensor_tensor(acc[:, t, :], acc[:, t, :], b[:, 0:D], ALU.add).then_inc(y_free, 1)
            v.sem_inc(xg_free, 1)
            dve.wait_ge(y_free, y.base + y.n + 2)
            for t in range(nt):
                m_ = mark(v.bn_stats(st[:, t, :], acc[:, t, :]))
            since(m_)
            dve.sem_inc(measured, 1)
            for t in range(nt):
                m_ = mark(v.bn_aggr(mv[:, t, :], st[:, t, :]))
            since(m_)
            v.tensor_scalar(rs[:, 0:nt], mv[:, 0:nt, 1:2].rearrange("p t o -> p (t o)"), LN_EPS, None, ALU.add).then_inc(var_in, 1)
            dve.wait_ge(var_sd, g + 1)
            link(v.reciprocal(rs[:, 0:nt], rs[:, 0:nt]))
            for t in range(nt):
                last = v.tensor_scalar(hg[:, t, :], acc[:, t, :], mv[:, t, 0:1], rs[:, t:t + 1], ALU.subtract, ALU.mult)
            last.then_inc(hg_ready, 1)
            hook("B1")
            b = full()
            lg = b[:, 0:nt * NE].rearrange("p (t e) -> p t e", e=NE)
            link(v.tensor_tensor(wg[:, 0:nt, :], lg, br_all[:, :].unsqueeze(1).to_broadcast([P, nt, NE]), ALU.add))
            dve.sem_inc(y_free, 1)
            link(v.reduce_max(mx[:, 0:nt], wg[:, 0:nt, :], AX.X))
            link(v.tensor_tensor(wg[:, 0:nt, :], wg[:, 0:nt, :], mx[:, 0:nt].unsqueeze(2).to_broadcast([P, nt, NE]), ALU.subtract))
            dve.sem_inc(sm_in, 1)
            dve.wait_ge(sm_exp, g + 1)
            link(v.reduce_sum(mx[:, 0:nt], wg[:, 0:nt, :], AX.X))
            link(v.reciprocal(mx[:, 0:nt], mx[:, 0:nt]))
            v.tensor_tensor(wg[:, 0:nt, :], wg[:, 0:nt, :], mx[:, 0:nt].unsqueeze(2).to_broadcast([P, nt, NE]),
                            ALU.mult).then_inc(wg_ready, 1)
            dve.wait_ge(wg_ready, g + 1)
            if nxt:
                norm_x(dve, g + 1, nxt, link)
            m_acc = {}
            for s in range(NE + 2):
                if s == 2:
                    for hf in range((nt + 1) // 2):
                        b = full()
                        w_ = min(nt - 2 * hf, 2) * P
                        last = v.tensor_copy(wT[:, hf * 2 * P:hf * 2 * P + w_], b[0:NE, 0:w_])
                        last.then_inc(y_free, 1)
                    dve.wait_ge(y_free, y.base + y.n + 2)
                    dve.sem_inc(wT_ready, 1)
                if s > 1:
                    e_ = s - 2
                    for hf in range((nt + 1) // 2):
                        b = full()
                        if hf in m_acc:
                            since(m_acc[hf])
                        for t in range(2 * hf, min(nt, 2 * hf + 2)):
                            last = v.scalar_tensor_tensor(out=acc[:, t, :], in0=b[:, (t % 2) * D:(t % 2 + 1) * D],
                                                          scalar=wg[:, t, e_:e_ + 1], in1=acc[:, t, :],
                                                          op0=ALU.mult, op1=ALU.add)
                            if t < min(nt, 2 * hf + 2) - 1:
                                continue
                            m_acc[hf] = mark(last)
                        since(m_acc[hf])
                        dve.sem_inc(y_free, 1)
                hook(f"s{s}")
            for hf in range((nt + 1) // 2):
                b = full()
                w_ = min(nt - 2 * hf, 2) * D
                o = acc[:, 2 * hf:min(nt, 2 * hf + 2), :].rearrange("p t d -> p (t d)")
                v.tensor_tensor(o, o, b[:, 0:w_], ALU.add).then_inc(y_free, 1)
            dve.wait_ge(y_free, y.base + y.n + 2)
            dve.sem_inc(out_ready, 1)
            assert not nxt or count[0] == per, count[0]

        PER = 1 + GT + 2 * GT + 1 + 5 + 2 + GT // 2 * NE

        SCAN = NSB * NW

        def each_group(eng, scan, emit):
            with eng.Fori(0, NG - 1) as g:
                scan(g, NW)
                emit(g, GT, 0, GT)
            scan(NG - 1, NWL)
            emit(NG - 1, LT, 1, 0)

        def branches(eng, fast, general):
            broken = eng.value_load(flag_i[0:1, 0:1], min_val=-NP, max_val=NP)
            with eng.If(broken > 0):
                general()
            with eng.Else():
                fast()

        with nc.Block() as block:
            @block.sync
            def _(sp):
                load_x(sp, 0, GT)
                sp.dma_start(xg[:, GT, :], a["x"][NG * T:NP, :]).then_inc(x_odd, 16)
                sp.sem_inc(out_stored, 16)
                with sp.Fori(0, NG - 1) as g:
                    grp_sp(sp, g, GT, GT)
                grp_sp(sp, NG - 1, LT, 0)
                sp.wait_ge(out_stored, 16 * (NG + 1) + 16)

            @block.gpsimd
            def _(pool):
                def fast():
                    for J in range(PRE, GS + LEAD):
                        sb_pool(pool, J, J, lambda s, b: (src, typ)[s][:, J * SB + b:J * SB + b + 1])
                    with pool.Fori(1, NG) as k:
                        for j in range(GS):
                            if j % HG == 0:
                                if j == 0:
                                    pool.wait_ge(idx_put, k * 2 - 1)
                                else:
                                    pool.wait_ge(idx_put, k * 2)
                            sb_pool(pool, k * GS + (LEAD + j), LEAD + j, lambda s, b: idx[:, j // HG, s, (j % HG) * SB + b:(j % HG) * SB + b + 1])

                    for J in range(NSB - REST, NSB):
                        sb_pool(pool, J, J, lambda s, b: (src, typ)[s][:, J * SB + b:J * SB + b + 1])

                def general():
                    for J in range(PRE):
                        pool.wait_ge(gath[J], 128)

                    def scan(g, nw):
                        with pool.Fori(0, NSB) as J:
                            pool.wait_ge(g_idx, g * NSB + J + 1)
                            pool.sem_inc(issued, 1)
                            for b in range(SB):
                                for tab, dst_, s in ((rtab, R, 1), (htab, H, 0)):
                                    pool.indirect_dma_start(
                                        out=dst_[:, 0, b * DX:(b + 1) * DX], out_offset=None, in_=tab,
                                        in_offset=bass.IndirectOffsetOnAxis(ap=idx[:, 0, s, b:b + 1], axis=0)).then_inc(g_gath, 16)

                    each_group(pool, scan, lambda g, nt, i, nxt: None)

                branches(pool, fast, general)

            @block.scalar
            def _(act):
                def fast():
                    split_hi(act, 0, 0)
                    for J in range(GS + LEAD):
                        sb_act(act, J, J)
                    with act.Fori(1, NG) as k:
                        hook = lambda p: p in POS and sb_act(act, k * GS + (LEAD + POS.index(p)), LEAD + POS.index(p))
                        grp_act(act, k - 1, GT, hook, (added, k * GS + (LEAD - 1)), GT, True)
                    for J in range(NSB - REST, NSB):
                        sb_act(act, J, J, J + 1 < NSB)
                    grp_act(act, NG - 1, LT, none, (added, NSB), 0)

                def general():
                    def scan(g, nw):
                        with act.Fori(0, NSB) as J:
                            act.wait_ge(prod, g * NSB + J + 1)
                            nc.scalar.activation(Xh[:, 0, :], H[:, 0, :], ACT.Copy).then_inc(hi_done, 1)
                            with act.Fori(0, nw) as w:
                                act.wait_ge(g_mm, g * SCAN + J * nw + w + 1)
                                nc.scalar.activation(Psb[:, 0, 0:D + 2], PA[0:W, 0:D + 2], ACT.Copy).then_inc(g_ev, 1)

                    each_group(act, scan, lambda g, nt, i, nxt: grp_act(act, g, nt, none, (g_add, g * SCAN + NSB * (NW if nxt else NWL)), nxt))

                z = Fill(0, ZF, 4)
                for k in range(2):
                    i, no = z.take()
                    act.wait_ge(z_full, no)
                    nc.scalar.activation(hT[:, k, :], Z[i][:, 0:TL], ACT.Copy).then_inc(z_free, 1)
                branches(act, fast, general)

            @block.tensor
            def _(pe):
                def fast():
                    for J in range(GS + LEAD):
                        sb_pe(pe, J, J)
                    with pe.Fori(1, NG) as k:
                        hook = lambda p: p in POS and sb_pe(pe, k * GS + (LEAD + POS.index(p)), LEAD + POS.index(p))
                        grp_pe(pe, k - 1, GT, hook, GT)
                    for J in range(NSB - REST, NSB):
                        sb_pe(pe, J, J)
                    sb_turn(pe, NSB - 1, NSB - 1)
                    grp_pe(pe, NG - 1, LT, none, 0)

                def general():
                    def scan(g, nw):
                        with pe.Fori(0, NSB) as J:
                            with pe.Fori(0, nw) as w:
                                at = g * SCAN + J * nw + w + 1
                                pe.wait_ge(g_s, at)
                                for b in range(SB):
                                    for x in (Xh, Xl):
                                        last = pe.matmul(PA[0:W, 0:D + 2], S[:, 0, b, :], x[:, 0, b * DX:b * DX + D + 2],
                                                         start=b == 0 and x is Xh, stop=b == SB - 1 and x is Xl)
                                last.then_inc(g_mm, 1)
                                pe.wait_ge(g_ev, at)
                                pe.sem_inc(turning, 1)
                                for k, (lo, hi) in enumerate(((0, P), (P, D), (D, D + 2))):
                                    last = pe.transpose(PT[0:hi - lo, k * W:(k + 1) * W], Psb[:, 0, lo:hi], ident[0:W, 0:W])
                                last.then_inc(g_tr, 1)

                    each_group(pe, scan, lambda g, nt, i, nxt: grp_pe(pe, g, nt, none, nxt))

                turn(pe, Fill(0, ZF, 4), LT, 1)
                branches(pe, fast, general)

            @block.vector
            def _(dve):
                v = nc.vector
                dve.sem_inc(z_free, 4)
                dve.sem_inc(y_free, 2)
                first = [0]

                def link(ins):
                    first[0] += 1
                    ins.then_inc(f_own[3], 1)
                    dve.wait_ge(f_own[3], first[0])

                link(v.memset(zeros[:, :, :], 0.0))
                norm_odd(dve, link)
                norm_x(dve, 0, GT, link)

                def fast():
                    dve.sem_inc(idx_put, 2)
                    sb_product(dve, 0, 0)
                    split_lo(dve, 0, 0)
                    for J in range(GS + LEAD):
                        sb_dve(dve, J, J)
                    with dve.Fori(1, NG) as k:
                        def hook(p):
                            if p not in POS:
                                return
                            j = POS.index(p)
                            J = k * GS + (LEAD + j)
                            sb_dve(dve, J, LEAD + j)
                            if j % HG == HG - 1:
                                hf = j // HG
                                for s, t in enumerate((src, typ)):
                                    last = v.tensor_copy(idx[:, hf, s, :], t[:, ds((k * GS + (LEAD + GS + HG * hf)) * SB, HG * SB)])
                                last.then_inc(idx_put, 1)

                        grp_dve(dve, k - 1, GT, hook, f_own[0], 0, PER, GT, True)
                    for J in range(NSB - REST, NSB):
                        sb_dve(dve, J, J, J + 1 < NSB)
                    sb_add(dve, NSB - 1, NSB - 1)
                    grp_dve(dve, NG - 1, LT, none, f_own[1], NG - 1, PER, 0)

                def general():
                    dl = dloc[:, 0:NB].rearrange("p (s b) -> p s b", b=SB)
                    link(v.tensor_tensor(dl, dl, PA[:, 0:NSB].unsqueeze(2).to_broadcast([P, NSB, SB]), ALU.add))
                    def scan(g, nw):
                        with dve.Fori(0, NSB) as J:
                            for s, t in enumerate((src, typ)):
                                last = v.tensor_copy(idx[:, 0, s, 0:SB], t[:, ds(J * SB, SB)])
                            last.then_inc(g_idx, 1)
                            dve.wait_ge(g_gath, (g * NSB + J) * 128 + 128)
                            v.tensor_tensor(H[:, 0, :], H[:, 0, :], R[:, 0, :], ALU.mult).then_inc(prod, 1)
                            dve.wait_ge(hi_done, g * NSB + J + 1)
                            v.tensor_tensor(Xl[:, 0, :], H[:, 0, :], Xh[:, 0, :].bitcast(fp32), ALU.subtract)
                            v.tensor_copy(dwin[:, :], dloc[:, ds(J * SB, SB)]).then_inc(g_own, 1)
                            with dve.Fori(0, nw) as w:
                                at = g * SCAN + J * nw + w + 1
                                dve.wait_ge(g_own, g * (NSB * (NW + 1) + 2) + J * (nw + 1) + w + 1)
                                v.tensor_tensor(S[:, 0, :, :], dwin[:, :].unsqueeze(2).to_broadcast([P, SB, W]),
                                                iota_w[:, :].unsqueeze(1).to_broadcast([P, SB, W]), ALU.is_equal).then_inc(g_s, 1)
                                dve.wait_ge(g_s, at)
                                v.tensor_scalar(dwin[:, :], dwin[:, :], float(-W), None, ALU.add).then_inc(g_own, 1)
                                dve.wait_ge(g_tr, at)
                                w_ = aggT[:, :, ds(w * W, W)]
                                v.tensor_tensor(w_, w_, PT[:, 0:2 * W].rearrange("p (k w) -> p k w", k=2), ALU.add)
                                c_ = aggC[:, ds(w * W, W)]
                                v.tensor_tensor(c_, c_, PT[0:2, 2 * W:3 * W], ALU.add).then_inc(g_add, 1)
                                dve.wait_ge(g_add, at)
                        v.tensor_scalar(dloc[:, 0:NB], dloc[:, 0:NB], float(-T), None, ALU.add).then_inc(g_own, 1)
                        dve.wait_ge(at_ready, g + 1)
                        v.memset(agg[:, :, :], 0.0).then_inc(g_own, 1)
                        dve.wait_ge(g_own, g * (NSB * (NW + 1) + 2) + NSB * (nw + 1) + 2)

                    each_group(dve, scan, lambda g, nt, i, nxt: grp_dve(dve, g, nt, none, f_own[i], i * (NG - 1), PER, nxt))

                branches(dve, fast, general)


def layout(x, src, dst, edge_type_500, L0_gnn_relation_emb, L0_gnn_msg_w, L0_gnn_msg_b, L0_gnn_upd_w,
           L0_gnn_upd_b, L0_gnn_gate_w, L0_gnn_gate_b, **f):
    n, e, nrel = x.shape[0], src.shape[0], L0_gnn_relation_emb.shape[0]
    nt, ng, nsb = sizes(n, e)
    nb = nsb * SB

    def cols(v, fill, wide):
        v = np.asarray(v)
        o = np.full(wide * P, fill, v.dtype)
        o[:e] = v
        return np.ascontiguousarray(o.reshape(wide, P).T)

    dst = np.asarray(dst)
    wide = nb + GS * SB
    x = np.asarray(x)
    xp = np.zeros((nt * P, D), x.dtype)
    xp[:n] = x
    at = ((0, 1, 2, 3), (1, 0, 3, 2), (2, 3, 0, 1), (3, 2, 1, 0))
    mw, uw = np.asarray(L0_gnn_msg_w), np.asarray(L0_gnn_upd_w)
    km = np.concatenate([np.concatenate([mw[i] for i in row], 1) for row in at], 0)
    u = np.concatenate([np.concatenate([uw[i] for i in row], 1) for row in at], 0)
    ut = u.T.reshape(D, 4, 64).transpose(0, 2, 1).reshape(D, D)
    g = {k[len("L0_ffn_"):]: np.asarray(v) for k, v in f.items()}
    bn = np.stack([np.stack([g[k + str(l)].reshape(NE * 2, P).T for k in ("b", "g", "be", "m", "v")], 1) for l in (1, 2)], 1)
    return {
        "x": xp, "src": cols(src, n, wide), "typ": cols(edge_type_500, nrel, wide), "dst": cols(dst, dst[-1], nb),
        "rel": np.asarray(L0_gnn_relation_emb),
        "gw": np.asarray(L0_gnn_gate_w).reshape(64, 4).T.reshape(D), "gb": np.asarray(L0_gnn_gate_b),
        "km": km, "ut": ut, "mb": np.asarray(L0_gnn_msg_b).reshape(2, P).T,
        "ub": np.asarray(L0_gnn_upd_b).T.reshape(D),
        "bn": bn, "wr": g["Wr"], "br": g["br"], "bo": g["bo"],
        "w1": g["W1"], "w2": g["W2"], "wo": g["Wo"],
    }, n, e, nrel


def kernel(**inputs):
    import concourse.bacc as bacc
    from concourse.bass_utils import run_bass_kernel_spmd

    data, n, e, nrel = layout(**inputs)
    nc = bacc.Bacc("TRN2", target_bir_lowering=False, num_devices=1)
    arrays = {f"in_{k}": np.ascontiguousarray(v) for k, v in data.items()}
    aps = {k[3:]: nc.dram_tensor(k, v.shape, mybir.dt.from_np(v.dtype), kind="ExternalInput").ap() for k, v in arrays.items()}
    out = nc.dram_tensor("out", (n, D), mybir.dt.float32, kind="ExternalOutput").ap()
    build(nc, aps, out, n, e, nrel)
    r = run_bass_kernel_spmd(nc, [arrays], core_ids=[0])
    return r.results[0]["out"]
```
